# Optimizing a Trainium2 kernel written in Bass

```python
import numpy as np
import jax
import jax.numpy as jnp

def _softmax(x, axis=-1):
    return jax.nn.softmax(x, axis=axis)

def _gelu(x):
    return jax.nn.gelu(x, approximate=True)

def _silu(x):
    return jax.nn.silu(x)

def _sigmoid(x):
    return jax.nn.sigmoid(x)

def _layernorm(x, axis=-1, eps=1e-05):
    m = jnp.mean(x, axis=axis, keepdims=True)
    v = jnp.var(x, axis=axis, keepdims=True)
    return (x - m) / jnp.sqrt(v + eps)

def _scatter_add(tgt, idx, src, axis=0):
    return tgt.at[idx].add(src)

def _segment_sum(src, seg, n):
    return jax.ops.segment_sum(src, seg, n)
kernel_name = 'mk_seq_preln_d1_jaxref_r4_11a00e'

def setup_inputs(seed: int=0):
    np.random.seed(seed)
    _w = jnp.asarray

    def _L0_attn_setup():
        import jax, jax.numpy as jnp
        import numpy as np
        D_MODEL = 1024
        NUM_HEADS = 32
        HEAD_DIM = D_MODEL // NUM_HEADS
        Q_LAT = 12
        KV_LAT = 4
        B, S = (2, 512)
        key = jax.random.key(seed)
        ks = jax.random.split(key, 6)
        sc = lambda fan_in: 1.0 / np.sqrt(fan_in)
        return {'x': jax.random.normal(ks[0], (B, S, D_MODEL), jnp.float32), 'Wq_d': jax.random.normal(ks[1], (D_MODEL, Q_LAT), jnp.float32) * sc(D_MODEL), 'bq_d': jnp.zeros((Q_LAT,), jnp.float32), 'W_qk': jax.random.normal(ks[2], (Q_LAT, NUM_HEADS * KV_LAT), jnp.float32) * sc(Q_LAT), 'b_qk': jnp.zeros((NUM_HEADS * KV_LAT,), jnp.float32), 'Wkv_d': jax.random.normal(ks[3], (D_MODEL, KV_LAT), jnp.float32) * sc(D_MODEL), 'bkv_d': jnp.zeros((KV_LAT,), jnp.float32), 'Wv_u': jax.random.normal(ks[4], (KV_LAT, NUM_HEADS * HEAD_DIM), jnp.float32) * sc(KV_LAT), 'bv_u': jnp.zeros((NUM_HEADS * HEAD_DIM,), jnp.float32), 'Wo': jax.random.normal(ks[5], (NUM_HEADS * HEAD_DIM, D_MODEL), jnp.float32) * sc(NUM_HEADS * HEAD_DIM), 'bo': jnp.zeros((D_MODEL,), jnp.float32)}
    _L0_attn_in = _L0_attn_setup()

    def _L0_ffn_setup():
        import jax, jax.numpy as jnp
        import numpy as np
        B_, S, D_IN, D_OUT = (4, 512, 1024, 1024)
        N, RANK, ALPHA = (8, 16, 32)
        SCALE = ALPHA / RANK
        key = jax.random.key(seed)
        kx, ka, kb, kw, kbias = jax.random.split(key, 5)
        x = jax.random.normal(kx, (B_, S, D_IN), dtype=jnp.float32)
        lora_A = jax.random.normal(ka, (N, RANK, D_IN), dtype=jnp.float32) * (1.0 / np.sqrt(D_IN))
        lora_B = jax.random.normal(kb, (N, D_OUT, RANK), dtype=jnp.float32) * (1.0 / np.sqrt(RANK))
        W = jax.random.normal(kw, (D_OUT, D_IN), dtype=jnp.float32) * (1.0 / np.sqrt(D_IN))
        bias = jax.random.normal(kbias, (D_OUT,), dtype=jnp.float32) * 0.01
        lora_weights = jnp.full((N,), 1.0 / N, dtype=jnp.float32)
        return {'x': x, 'lora_A': lora_A, 'lora_B': lora_B, 'W': W, 'bias': bias, 'lora_weights': lora_weights}
    _L0_ffn_in = _L0_ffn_setup()
    _d = {'L0_attn_x': _L0_attn_in['x'], 'L0_attn_Wq_d': _L0_attn_in['Wq_d'], 'L0_attn_bq_d': _L0_attn_in['bq_d'], 'L0_attn_W_qk': _L0_attn_in['W_qk'], 'L0_attn_b_qk': _L0_attn_in['b_qk'], 'L0_attn_Wkv_d': _L0_attn_in['Wkv_d'], 'L0_attn_bkv_d': _L0_attn_in['bkv_d'], 'L0_attn_Wv_u': _L0_attn_in['Wv_u'], 'L0_attn_bv_u': _L0_attn_in['bv_u'], 'L0_attn_Wo': _L0_attn_in['Wo'], 'L0_attn_bo': _L0_attn_in['bo'], 'L0_ffn_lora_A': _L0_ffn_in['lora_A'], 'L0_ffn_lora_B': _L0_ffn_in['lora_B'], 'L0_ffn_W': _L0_ffn_in['W'], 'L0_ffn_bias': _L0_ffn_in['bias'], 'L0_ffn_lora_weights': _L0_ffn_in['lora_weights']}
    _x0 = _d['L0_attn_x']
    _d['L0_attn_x'] = jax.random.normal(jax.random.fold_in(jax.random.key(seed), 1), (2, 2048, 1024), dtype=_x0.dtype)
    del _x0
    return _d

def reference(L0_attn_x, L0_attn_Wq_d, L0_attn_bq_d, L0_attn_W_qk, L0_attn_b_qk, L0_attn_Wkv_d, L0_attn_bkv_d, L0_attn_Wv_u, L0_attn_bv_u, L0_attn_Wo, L0_attn_bo, L0_ffn_lora_A, L0_ffn_lora_B, L0_ffn_W, L0_ffn_bias, L0_ffn_lora_weights):

    def _L0_attn_ref(x, Wq_d, bq_d, W_qk, b_qk, Wkv_d, bkv_d, Wv_u, bv_u, Wo, bo):
        import jax, jax.numpy as jnp
        import numpy as np
        D_MODEL = 1024
        NUM_HEADS = 32
        HEAD_DIM = D_MODEL // NUM_HEADS
        Q_LAT = 12
        KV_LAT = 4
        B, S = (2, 512)
        b, s, _ = x.shape
        C_q = x @ Wq_d + bq_d
        C_kv = x @ Wkv_d + bkv_d
        q = (C_q @ W_qk + b_qk).reshape(b, s, NUM_HEADS, KV_LAT)
        scores = jnp.einsum('bqhd,bkd->bhqk', q, C_kv) / jnp.sqrt(jnp.asarray(KV_LAT, x.dtype))
        attn = jax.nn.softmax(scores, axis=-1)
        V = (C_kv @ Wv_u + bv_u).reshape(b, s, NUM_HEADS, HEAD_DIM)
        out = jnp.einsum('bhqk,bkhd->bqhd', attn, V).reshape(b, s, NUM_HEADS * HEAD_DIM)
        return out @ Wo + bo

    def _L0_ffn_ref(x, lora_A, lora_B, W, bias, lora_weights):
        import jax, jax.numpy as jnp
        import numpy as np
        B_, S, D_IN, D_OUT = (4, 512, 1024, 1024)
        N, RANK, ALPHA = (8, 16, 32)
        SCALE = ALPHA / RANK
        h = jnp.einsum('bsd,nrd->nbsr', x, lora_A)
        coef = (SCALE * lora_weights)[:, None, None]
        lora_out = jnp.einsum('nbsr,nor->bso', h, lora_B * coef)
        base = jnp.einsum('bsd,od->bso', x, W) + bias
        return base + lora_out
    x = L0_attn_x
    x = x + _L0_attn_ref(_layernorm(x, axis=-1), L0_attn_Wq_d, L0_attn_bq_d, L0_attn_W_qk, L0_attn_b_qk, L0_attn_Wkv_d, L0_attn_bkv_d, L0_attn_Wv_u, L0_attn_bv_u, L0_attn_Wo, L0_attn_bo)
    x = x + _L0_ffn_ref(_layernorm(x, axis=-1), L0_ffn_lora_A, L0_ffn_lora_B, L0_ffn_W, L0_ffn_bias, L0_ffn_lora_weights)
    return x

_drawn_inputs = setup_inputs


def setup_inputs(seed=0):
    import zlib

    import numpy as np

    out = dict(_drawn_inputs(seed))
    spreads = {'L0_attn_bq_d': (0.0, 0.1),
     'L0_attn_b_qk': (0.0, 0.1),
     'L0_attn_bkv_d': (0.0, 0.1),
     'L0_attn_bv_u': (0.0, 0.1),
     'L0_attn_bo': (0.0, 0.1),
     'L0_ffn_lora_weights': (0.125, 0.2)}
    factors = {'L0_ffn_bias': 8.0}
    for name, (base, spread) in spreads.items():
        noise = np.random.default_rng([zlib.crc32(name.encode()), seed]).standard_normal(out[name].shape)
        drawn = base * np.exp(spread * noise) if base else spread * noise
        out[name] = jnp.asarray(drawn.astype(out[name].dtype))
    for name, factor in factors.items():
        out[name] = (out[name] * factor).astype(out[name].dtype)
    return out
```

```python
from contextlib import ExitStack

import concourse.bass as bass
from concourse import mybir

F32 = mybir.dt.float32
BF16 = mybir.dt.bfloat16
I32 = mybir.dt.int32
ALU = mybir.AluOpType
ACT = mybir.ActivationFunctionType
AX = mybir.AxisListType

P = 128
N = 512


def build_block(nc, x, wq_d, bq_d, w_qk, b_qk, wkv_d, bkv_d, wv_u, bv_u, wo, bo,
                lora_a, lora_b, w_ffn, bias_ffn, lora_w, out):
    B, S, D = x.shape
    QL = wq_d.shape[1]
    L = wkv_d.shape[1]
    H = w_qk.shape[1] // L
    HD = wv_u.shape[1] // H
    NL, RANK = lora_a.shape[0], lora_a.shape[1]
    LORA_SCALE = 2.0
    EPS = 1e-5
    SCALE = L ** -0.5
    BOUND_LIMIT = 30.0
    T = B * S
    CHUNKS = T // N
    CB = S // N
    TT = N // P
    KT = S // P
    KB = D // P
    G4 = H // 4
    W5 = L + 1
    PARTS = 3
    ROWS = PARTS * W5
    QROW = 96
    assert H * L == P and NL * RANK == P and D == 2 * N and HD == 32

    x_t = x.rearrange("b s d -> (b s) d").rearrange("(t p) d -> t p d", p=P)
    out_t = out.rearrange("b s d -> (b s) d").rearrange("(t p) d -> t p d", p=P)
    qd = nc.dram_tensor("q_parts", [H, ROWS, T], BF16, kind="Internal").ap()

    with ExitStack() as ctx:
        def sb(name, shape, dt):
            return ctx.enter_context(nc.sbuf_tensor(name, shape, dt))

        def sem(name):
            return ctx.enter_context(nc.semaphore(name))

        ps = ctx.enter_context(nc.psum_tensor("ps", [P, 8, N], F32))

        ident = sb("ident", [P, P], F32)
        ones = sb("ones", [P, P], F32)
        head_of_row = sb("head_of_row", [P, H], F32)
        w_down = sb("w_down", [P, KB, P], F32)
        down_bias = sb("down_bias", [P, 1], F32)
        wqk_sb = sb("wqk_sb", [P, P], F32)
        bqk_sb = sb("bqk_sb", [P, 1], F32)
        sel_latent = sb("sel_latent", [P, P], F32)
        w_vo = sb("w_vo", [P, D], F32)
        attn_bias = sb("attn_bias", [P, D], F32)
        ffn_bias = sb("ffn_bias", [P, D], F32)
        w_eff = sb("w_eff", [P, KB, D], F32)
        key_t = sb("key_t", [P, T], BF16)
        c_aug = sb("c_aug", [P, T // P, 32], F32)
        q_f32 = sb("q_f32", [P, T], F32)
        q_in = sb("q_in", [P, 2, 4, N], BF16)
        probs = sb("probs", [P, 2, 4 * N], F32)
        o_sb = sb("o_sb", [P, N], F32)
        o_q = sb("o_q", [P, TT, H * L], F32)
        o_t = sb("o_t", [P, N], F32)
        recip = sb("recip", [P, TT, 4], F32)
        xt = sb("xt", [P, 2, TT, D], F32)
        xn = sb("xn", [P, TT, D], F32)
        xn_t = sb("xn_t", [P, KB, N], F32)
        stats = sb("stats", [P, TT, 2, 6], F32)
        mv = sb("mv", [P, TT, 2], F32)
        nw = sb("nw", [P, 4, TT], F32)
        lat = sb("lat", [P, N], F32)
        part_f = sb("part_f", [P, 2, N], F32)
        part_b = sb("part_b", [P, 2, N], BF16)
        q_parts = sb("q_parts_sb", [P, PARTS, N], BF16)
        c_max = sb("c_max", [P, CHUNKS], F32)
        c_maxb = sb("c_maxb", [P, B], F32)
        bound_w = sb("bound_w", [P, B, H], F32)
        small = sb("small", [P, 512], F32)
        shift_min = sb("shift_min", [H, CHUNKS + 1], F32)
        tight_f = sb("tight_f", [1, H + 1], F32)
        tight = sb("tight", [1, 1], I32)
        row_max = sb("row_max", [P, TT, H], F32)

        wv_in = sb("wv_in", [L, D], F32)

        y = xt[:, 0]
        w_stage = xn
        lv = xt[:, 1, 0, :].rearrange("p (g m) -> p g m", g=G4)
        lora_bt = xt[:, 1, 1, :]
        lora_a_sb = xt[:, 1, 2, :]
        lora_b_sb = xt[:, 1, 3, :].rearrange("p (a n r) -> p a n r", a=KB, n=NL)
        bv_wide = xn_t[:, 0:2, :].rearrange("p a (g m) -> p (a g) m", m=P)
        wkv_in = small[:, 0:KB * L].rearrange("p (k n) -> p k n", k=KB)
        wq_in = small[:, 32:32 + KB * QL].rearrange("p (k n) -> p k n", k=KB)
        coef = small[:, 136:137]
        wvbv_t = small[:, 144:144 + G4 * L + G4]
        wv_t = wvbv_t[:, 0:G4 * L].rearrange("p (g n) -> p g n", g=G4)
        bv_col = wvbv_t[:, G4 * L:G4 * L + G4]
        bias_row = small[0:1, 192:192 + P]
        bkv_row = small[0:1, 320:320 + L]
        shift = part_f[0:H, 0, :]
        shift_r = part_f[0:H, 1, :]
        bq_row = small[0:1, 330:330 + QL]
        bv_rows = small[0:G4, 384:384 + P]

        w_in = sem("w_in")
        lora_in = sem("lora_in")
        stage_in = sem("stage_in")
        stage_used = sem("stage_used")
        const_ok = sem("const_ok")
        pool_zero = sem("pool_zero")
        q_zero = sem("q_zero")
        bias_ps = sem("bias_ps")
        down_ok = sem("down_ok")
        v_set, v_ln, v_lat, v_shift, v_rec = (sem(n) for n in ("v_set", "v_ln", "v_lat", "v_shift", "v_rec"))
        prep_ps = sem("prep_ps")
        prep_ok = sem("prep_ok")
        x_in = [sem("x_in0"), sem("x_in1")]
        xn_ready = sem("xn_ready")
        t_ready = sem("t_ready")
        t_moved = sem("t_moved")
        down_done = sem("down_done")
        lat_ready = sem("lat_ready")
        q_ps = sem("q_ps")
        caug_ps = sem("caug_ps")
        caug_ready = sem("caug_ready")
        lat_split = sem("lat_split")
        q_read = sem("q_read")
        q_split = sem("q_split")
        q_stored = sem("q_stored")
        abs_ready = sem("abs_ready")
        bound_w_ps = sem("bound_w_ps")
        bound_w_ready = sem("bound_w_ready")
        bound_ps = sem("bound_ps")
        shift_split = sem("shift_split")
        shift_stored = sem("shift_stored")
        min_ready = sem("min_ready")
        tight_ps = sem("tight_ps")
        tight_ok = sem("tight_ok")
        m_loaded = sem("m_loaded")
        m_scores = sem("m_scores")
        m_max = sem("m_max")
        m_abs = sem("m_abs")
        m_used = sem("m_used")
        m_sum_ps = sem("m_sum_ps")
        m_split = sem("m_split")
        m_read = sem("m_read")
        m_stored = sem("m_stored")
        q_loaded = [sem("q_loaded0"), sem("q_loaded1")]
        s_ready = sem("s_ready")
        exp_done = sem("exp_done")
        pv_done = sem("pv_done")
        o_moved = sem("o_moved")
        o_turned = sem("o_turned")
        o_normed = sem("o_normed")
        o_back = sem("o_back")
        o_t_ready = sem("o_t_ready")
        proj_ready = sem("proj_ready")
        y_ready = sem("y_ready")
        ffn_ready = sem("ffn_ready")
        ffn_moved = sem("ffn_moved")
        x_back = sem("x_back")
        xb_ready = sem("xb_ready")
        yb_ready = sem("yb_ready")
        out_done = sem("out_done")

        block = ctx.enter_context(nc.Block())

        W_IN = 11 * 16
        PAIRS = 2 * KT
        START = 1
        START_AT_1 = (t_moved, lat_ready, caug_ready, q_read, lat_split, caug_ps, q_ps, bound_ps, shift_split, q_stored,
                      shift_stored, t_ready, ffn_moved, y_ready, proj_ready, o_back, ffn_ready)
        PREP_PS_LORA, PREP_PS_VO, PREP_PS_BIAS = 3, 5, 7
        PREP_LORA, PREP_BV, PREP_VO, PREP_BIAS = 4, 5, 7, 9
        PREP_ALL = PREP_BIAS + 2 * KB

        @block.sync
        def _(sp):
            for s in START_AT_1:
                sp.sem_inc(s, START)
            sp.dma_start(wkv_in, wkv_d.rearrange("(k p) n -> p k n", p=P)).then_inc(w_in, 16)
            sp.dma_start(wq_in, wq_d.rearrange("(k p) n -> p k n", p=P)).then_inc(w_in, 16)
            sp.dma_start(wqk_sb[QROW:QROW + QL, :], w_qk).then_inc(w_in, 16)
            sp.dma_start(bq_row, bq_d.rearrange("(a n) -> a n", a=1)).then_inc(w_in, 16)
            sp.dma_start(bkv_row, bkv_d.rearrange("(a n) -> a n", a=1)).then_inc(w_in, 16)
            sp.dma_start(bqk_sb[:, :], b_qk.rearrange("(p a) -> p a", a=1)).then_inc(w_in, 16)
            sp.dma_start(bv_rows, bv_u.rearrange("(g p) -> g p", p=P)).then_inc(w_in, 16)
            sp.dma_start(wv_in[:, :], wv_u).then_inc(w_in, 16)
            sp.dma_start(attn_bias[:, :], bo.rearrange("(a n) -> a n", a=1).to_broadcast([P, D])).then_inc(w_in, 16)
            sp.dma_start(ffn_bias[:, :], bias_ffn.rearrange("(a n) -> a n", a=1).to_broadcast([P, D])).then_inc(w_in, 16)
            sp.dma_start(coef, lora_w.rearrange("(n a b) -> n a b", a=1, b=1).to_broadcast([NL, RANK, 1])
                         ).then_inc(w_in, 16)
            for half in range(2):
                for t in range(TT):
                    sp.dma_start(xt[:, half, t, :], x_t[half * TT + t]).then_inc(x_in[half], 16)
            def store_q(c):
                sp.wait_ge(q_split, c + 1)
                for k in range(PARTS):
                    sp.dma_start(qd[:, k * W5:k * W5 + L, bass.ds(c * N, N)], q_parts[:, k, :]).then_inc(q_stored, 16)

            with sp.Fori(0, CHUNKS // 2 - 1) as i:
                for half in range(2):
                    c = i * 2 + half
                    sp.wait_ge(xn_ready, (c + 1) * TT)
                    for t in range(TT):
                        sp.dma_start(xt[:, half, t, :], x_t[(c + 2) * TT + t]).then_inc(x_in[half], 16)
                    store_q(c)
            for c in range(CHUNKS - 2, CHUNKS):
                store_q(c)
            with sp.Fori(0, CHUNKS) as c:
                sp.wait_ge(shift_split, START + c + 1)
                for k in range(PARTS):
                        sp.dma_start(qd[:, k * W5 + L, bass.ds(c * N, N)], q_parts[0:H, k, :]).then_inc(shift_stored, 16)
            def load_q(c, g, slot, done):
                src = qd[bass.ds(g * 4, 4), :, bass.ds(c * N, N)].rearrange("h r n -> r h n")
                for j in range(PARTS):
                    sp.dma_start(q_in[32 * j:32 * j + ROWS, slot], src).then_inc(done, 16)

            sp.wait_ge(q_stored, START + 16 * PARTS * CHUNKS)
            sp.wait_ge(shift_stored, START + 16 * PARTS * CHUNKS)
            sp.wait_ge(q_zero, 1)
            sp.wait_ge(tight_ok, 1)
            with sp.If(sp.value_load(tight[:, :], min_val=0, max_val=1) < 1):
                with sp.Fori(0, CHUNKS) as c:
                    with sp.Fori(0, G4) as g:
                        load_q(c, g, 0, m_loaded)
                        sp.wait_ge(m_read, 1)
                        sp.sem_inc(m_read, -1)
                    sp.wait_ge(m_split, c + 1)
                    for k in range(PARTS):
                        sp.dma_start(qd[:, k * W5 + L, bass.ds(c * N, N)], q_parts[0:H, k, :]).then_inc(m_stored, 16)
                    sp.wait_ge(m_stored, PARTS * 16)
                    sp.sem_inc(m_stored, -PARTS * 16)

            sp.wait_ge(bound_ps, START + CHUNKS)
            sp.wait_ge(t_ready, START + CHUNKS * KB)
            sp.dma_start(lora_a_sb, lora_a.rearrange("n r d -> (n r) d")).then_inc(lora_in, 16)
            for a in range(KB):
                sp.dma_start(lora_b_sb[:, a], lora_b[:, a * P:(a + 1) * P, :].rearrange("n o r -> o n r")
                             ).then_inc(lora_in, 16)
            for k, (src, half) in enumerate(((wo, 0), (wo, 1), (wo, 0), (w_ffn, 0), (w_ffn, 1))):
                if k in (1, 2):
                    sp.wait_ge(stage_used, k)
                elif k:
                    sp.wait_ge(prep_ps, PREP_PS_BIAS if k == 3 else PREP_PS_BIAS + KB)
                sp.dma_start(w_stage[:, :, :], src[half * 4 * P:(half + 1) * 4 * P, :].rearrange("(a p) n -> p a n", p=P)
                             ).then_inc(stage_in, 16)
            def load_x(c):
                sp.wait_ge(out_done, c * TT * 16)
                for t in range(TT):
                    sp.dma_start(y[:, t, :], x_t[c * TT + t]).then_inc(x_back, 16)

            def store_out(p, t):
                sp.wait_ge(ffn_moved, START + (p * TT + t + 1) * 2)
                sp.dma_start(out_t[p * TT + t], y[:, t, :]).then_inc(out_done, 16)

            def beside_attention(c, first, last):
                for g in range(G4):
                    sp.wait_ge(s_ready, PAIRS * (c * G4 + g))
                    if g < G4 - 1:
                        load_q(c, g + 1, (g + 1) % 2, q_loaded[(g + 1) % 2])
                    elif not last:
                        load_q(c + 1, 0, 0, q_loaded[0])
                    if not first and 3 <= g < 3 + TT:
                        store_out(c - 1, g - 3)
                load_x(c)

            load_q(0, 0, 0, q_loaded[0])
            beside_attention(0, True, False)
            with sp.Fori(1, CHUNKS - 1) as c:
                beside_attention(c, False, False)
            beside_attention(CHUNKS - 1, False, True)
            for t in range(TT):
                store_out(CHUNKS - 1, t)
            sp.wait_ge(out_done, CHUNKS * TT * 16)

        @block.gpsimd
        def _(pool):
            pool.memset(ident[:, :], 0.0).then_inc(pool_zero, 1)
            pool.wait_ge(pool_zero, 1)
            pool.affine_select(out=ident[:, :], in_=ident[:, :], compare_op=ALU.not_equal, fill=1.0, base=0,
                               pattern=[[-1, P]], channel_multiplier=1).then_inc(const_ok, 1)
            pool.memset(ones[:, :], 1.0).then_inc(const_ok, 1)
            pool.memset(w_down[:, :, :], 0.0).then_inc(const_ok, 1)
            pool.memset(key_t[:, :], 0.0).then_inc(const_ok, 1)
            pool.memset(q_in[:, :, :, :], 0.0).then_inc(q_zero, 1)
            pool.wait_ge(prep_ok, PREP_BIAS)
            with pool.Fori(0, CHUNKS) as c:
                pool.wait_ge(x_back, (c + 1) * TT * 16)
                for t in range(TT):
                    pool.tensor_tensor(y[:, t, :], y[:, t, :], attn_bias[:, :], ALU.add).then_inc(xb_ready, 1)
                for t in range(TT):
                    pool.wait_ge(xn_ready, (CHUNKS + c) * TT + t + 1)
                    pool.tensor_tensor(y[:, t, :], y[:, t, :], ffn_bias[:, :], ALU.add).then_inc(yb_ready, 1)

        @block.scalar
        def _(act):
            act.sem_inc(down_done, KB)
            act.wait_ge(down_ok, 2)
            with act.Fori(0, CHUNKS) as c:
                for kb in range(KB):
                    act.wait_ge(t_ready, START + c * KB + kb + 1)
                    act.wait_ge(down_done, c * KB + kb + 1)
                    nc.scalar.activation(xn_t[:, kb, :], ps[:, kb % 4, :], ACT.Copy).then_inc(t_moved, 1)
                act.wait_ge(down_done, (c + 2) * KB)
                act.wait_ge(lat_split, START + c)
                act.wait_ge(caug_ps, START + c)
                act.wait_ge(q_ps, START + c)
                nc.scalar.activation(lat[:, :], ps[:, 4, :], ACT.Identity, bias=down_bias[:, 0:1]).then_inc(lat_ready, 1)
                act.wait_ge(caug_ps, START + c + 1)
                nc.scalar.activation(c_aug[:, bass.ds(c * TT, TT), :],
                                     ps[:, 6, :].rearrange("p (t m) -> p t m", t=TT)[:, :, 0:32], ACT.Copy
                                     ).then_inc(caug_ready, 1)
            act.wait_ge(lat_split, START + CHUNKS)
            act.wait_ge(q_ps, START + CHUNKS)
            with act.Fori(0, CHUNKS) as c:
                act.wait_ge(q_read, START + CHUNKS)
                act.wait_ge(bound_ps, START + c)
                nc.scalar.activation(lat[:, :], q_f32[:, bass.ds(c * N, N)], ACT.Abs).then_inc(abs_ready, 1)
            act.wait_ge(tight_ok, 1)
            with act.If(act.value_load(tight[:, :], min_val=0, max_val=1) < 1):
                with act.Fori(0, CHUNKS) as c:
                    nc.scalar.activation(lat[:, :], q_f32[:, bass.ds(c * N, N)], ACT.Abs).then_inc(m_abs, 1)
                    act.wait_ge(m_used, 1)
                    act.sem_inc(m_used, -1)
            act.wait_ge(prep_ok, PREP_ALL)

            def exps(c, first):
                for g in range(G4):
                    for kt in range(KT):
                        for pair in range(2):
                            act.wait_ge(s_ready, (c * G4 + g) * PAIRS + 2 * kt + pair + 1)
                            if pair == 0 and not (first and g == 0 and kt < 2):
                                act.wait_ge(pv_done, (c * G4 + g) * KT + kt - 1)
                            nc.scalar.activation(probs[:, kt % 2, bass.ts(pair, 2 * N)],
                                                 ps[:, 2 * pair:2 * pair + 2, :].rearrange("p a n -> p (a n)"),
                                                 ACT.Exp).then_inc(exp_done, 1)

            exps(0, True)
            with act.Fori(1, CHUNKS) as c:
                exps(c, False)

        @block.tensor
        def _(pe):
            pe.wait_ge(w_in, W_IN)
            pe.wait_ge(const_ok, 4)
            pe.wait_ge(down_ok, 1)
            nc.tensor.matmul(ps[:, 7, 0:1], bias_row, ones[0:1, 0:1], start=True, stop=True).then_inc(bias_ps, 1)
            pe.wait_ge(down_ok, 2)

            with pe.Fori(0, CHUNKS) as c:
                pe.wait_ge(xn_ready, (c + 1) * TT)
                for kb in range(KB + 2):
                    if kb < KB:
                        if kb >= 4:
                            pe.wait_ge(t_moved, START + c * KB + kb - 3)
                        elif kb == 0:
                            pe.wait_ge(t_moved, START + c * KB)
                        for t in range(TT):
                            last = nc.tensor.transpose(ps[:, kb % 4, bass.ts(t, P)], xn[:, t, bass.ts(kb, P)], ident[:, :])
                        last.then_inc(t_ready, 1)
                    if kb >= 2:
                        k = kb - 2
                        pe.wait_ge(t_moved, START + c * KB + k + 1)
                        if k == 0:
                            pe.wait_ge(lat_ready, START + c)
                        nc.tensor.matmul(ps[:, 4, :], w_down[:, k, :], xn_t[:, k, :], start=(k == 0), stop=(k == KB - 1)
                                         ).then_inc(down_done, 1)
                pe.wait_ge(lat_ready, START + c + 1)
                pe.wait_ge(caug_ready, START + c)
                for t in range(TT):
                    last = nc.tensor.transpose(ps[:, 6, bass.ts(t, P)], lat[:, bass.ts(t, P)], ident[:, :])
                last.then_inc(caug_ps, 1)
                pe.wait_ge(q_read, START + c)
                nc.tensor.matmul(ps[:, 5, :], wqk_sb[QROW:QROW + QL, :], lat[QROW:QROW + QL, :], start=True, stop=True
                                 ).then_inc(q_ps, 1)

            pe.wait_ge(caug_ready, START + CHUNKS)
            for b in range(B):
                pe.wait_ge(bound_w_ready, 2 * b + 1)
                nc.tensor.matmul(ps[:, 7, b:b + 1], sel_latent[:, :], c_maxb[:, b:b + 1], start=True, stop=True
                                 ).then_inc(bound_w_ps, 1)
                pe.wait_ge(bound_w_ready, 2 * b + 2)
                with pe.Fori(b * CB, (b + 1) * CB) as c:
                    pe.wait_ge(abs_ready, c + 1)
                    pe.wait_ge(shift_split, START + c)
                    nc.tensor.matmul(ps[0:H, 6, :], bound_w[:, b, :], lat[:, :], start=True, stop=True).then_inc(bound_ps, 1)

            pe.wait_ge(shift_split, START + CHUNKS)
            pe.wait_ge(min_ready, 1)
            nc.tensor.matmul(ps[0:1, 7, 0:H], shift_min[:, CHUNKS:CHUNKS + 1], ident[0:H, 0:H], start=True, stop=True
                             ).then_inc(tight_ps, 1)
            pe.wait_ge(tight_ok, 1)
            with pe.If(pe.value_load(tight[:, :], min_val=0, max_val=1) < 1):
                for b in range(B):
                    with pe.Fori(b * CB, (b + 1) * CB) as c:
                        with pe.Fori(0, G4):
                            pe.wait_ge(m_loaded, PARTS * 16)
                            pe.sem_inc(m_loaded, -PARTS * 16)
                            for u in range(4 * TT):
                                if u >= 2:
                                    pe.wait_ge(m_max, u - 1)
                                for n in range(KT // 4):
                                    last = nc.tensor.matmul(ps[:, 4 * (u % 2) + n, :],
                                                            q_in[:, 0, u // TT, bass.ts(u % TT, P)],
                                                            key_t[:, b * S + n * N:b * S + (n + 1) * N], start=True, stop=True)
                                last.then_inc(m_scores, 1)
                            pe.wait_ge(m_max, 4 * TT)
                            pe.sem_inc(m_max, -4 * TT)
                            pe.drain().then_inc(m_read, 1)
                        pe.wait_ge(m_abs, 1)
                        pe.sem_inc(m_abs, -1)
                        nc.tensor.matmul(ps[0:H, 6, :], bound_w[:, b, :], lat[:, :], start=True, stop=False).then_inc(m_used, 1)
                        for t in range(TT):
                            last = nc.tensor.matmul(ps[0:H, 6, bass.ts(t, P)], row_max[:, t, :], ident[:, :],
                                                    start=False, stop=(t == TT - 1))
                        last.then_inc(m_sum_ps, 1)
                        pe.wait_ge(m_split, c + 1)
            for g in range(G4):
                nc.tensor.transpose(ps[:, 6, bass.ts(g, L)], wv_in[:, bass.ts(g, P)], ident[0:L, 0:L])
            nc.tensor.transpose(ps[:, 6, G4 * L:G4 * L + G4], bv_rows, ident[0:G4, 0:G4]).then_inc(prep_ps, 1)
            pe.wait_ge(lora_in, (KB + 1) * 16)
            for half in range(2):
                if half == 1:
                    pe.wait_ge(prep_ok, 1)
                for a in range(4):
                    last = nc.tensor.transpose(ps[:, 7 - half, bass.ts(a, P)],
                                               lora_b_sb[:, half * 4 + a].rearrange("p n r -> p (n r)"), ident[:, :])
                last.then_inc(prep_ps, 1)
            pe.wait_ge(prep_ok, PREP_LORA)
            for half in range(2):
                pe.wait_ge(stage_in, (half + 1) * 16)
                for g in range(4):
                    for n in range(2):
                        last = nc.tensor.matmul(ps[:, 6 + n, :], lv[:, half * 4 + g, :], w_stage[:, g, bass.ts(n, N)],
                                                start=(half + g == 0), stop=(half == 1 and g == 3))
                        if half == 1 and g == 3:
                            last.then_inc(prep_ps, 1)
                if half == 0:
                    last.then_inc(stage_used, 1)
            pe.wait_ge(prep_ok, PREP_VO)
            for half in (1, 0):
                if half == 0:
                    pe.wait_ge(stage_in, 3 * 16)
                for g in range(4):
                    for n in range(2):
                        last = nc.tensor.matmul(ps[:, 6 + n, :], bv_wide[:, half * 4 + g, :], w_stage[:, g, bass.ts(n, N)],
                                                start=(half == 1 and g == 0), stop=(half == 0 and g == 3))
                        if half == 0 and g == 3:
                            last.then_inc(prep_ps, 1)
                if half == 1:
                    last.then_inc(stage_used, 1)
            pe.wait_ge(prep_ok, PREP_BIAS)
            for half in range(2):
                pe.wait_ge(stage_in, (4 + half) * 16)
                for kb in range(KB):
                    k = half * KB + kb
                    if k >= 2:
                        pe.wait_ge(prep_ok, PREP_BIAS + k - 1)
                    for a in range(4):
                        nc.tensor.matmul(ps[:, 6 + kb % 2, bass.ts(a, P)], w_stage[:, a, bass.ts(kb, P)], ident[:, :],
                                         start=(a == 0), stop=False)
                    last = nc.tensor.matmul(ps[:, 6 + kb % 2, :], lora_a_sb[:, bass.ts(kb, P)], lora_bt[:, bass.ts(half, N)],
                                            start=False, stop=True)
                    last.then_inc(prep_ps, 1)
            pe.wait_ge(prep_ok, PREP_ALL)

            def scores(c, b, g, kt, pair, first):
                if not (first and g == 0 and kt == 0):
                    pe.wait_ge(exp_done, (c * G4 + g) * PAIRS + 2 * kt + pair - 1)
                for h in (2 * pair, 2 * pair + 1):
                    last = nc.tensor.matmul(ps[:, h, :], key_t[:, bass.ts(b * KT + kt, P)], q_in[:, g % 2, h, :],
                                            start=True, stop=True)
                last.then_inc(s_ready, 1)

            def values(c, b, g, kt):
                pe.wait_ge(exp_done, (c * G4 + g) * PAIRS + 2 * kt + 2)
                for h in range(4):
                    last = nc.tensor.matmul(ps[32 * h:32 * h + 32, 4 + g % 2, :], c_aug[:, b * KT + kt, :],
                                            probs[:, kt % 2, bass.ts(h, N)], start=(kt == 0), stop=(kt == KT - 1))
                last.then_inc(pv_done, 1)

            def turn_o(c, g, post):
                pe.wait_ge(o_moved, c * G4 + g)
                pe.wait_ge(o_normed, c * G4 + g - 1)
                if post and g == 1:
                    pe.wait_ge(y_ready, START + c * TT * 2)
                elif post and g == 2:
                    pe.wait_ge(t_moved, START + (CHUNKS + c) * KB)
                elif post and 3 <= g <= 6:
                    pe.wait_ge(ffn_moved, START + ((c - 1) * TT + g - 2) * 2)
                for t in range(TT):
                    last = nc.tensor.transpose(ps[:, 7, bass.ts(t, P)], o_sb[:, bass.ts(t, P)], ident[:, :])
                last.then_inc(o_turned, 1)

            def turn_back(p):
                pe.wait_ge(o_normed, (p + 1) * G4)
                pe.wait_ge(ffn_moved, START + p * 2 * TT)
                for t in range(TT):
                    last = nc.tensor.transpose(ps[:, 6, bass.ts(t, P)], o_q[:, t, :], ident[:, :])
                last.then_inc(o_back, 1)

            def project(p, t):
                pe.wait_ge(o_t_ready, p + 1)
                pe.wait_ge(y_ready, START + (p * TT + t) * 2)
                for n in range(2):
                    nc.tensor.matmul(ps[:, 6 + n, :], o_t[:, bass.ts(t, P)], w_vo[:, bass.ts(n, N)], start=True, stop=True
                                     ).then_inc(proj_ready, 1)

            def turn_xn(p, kb, normed):
                pe.wait_ge(xn_ready, (CHUNKS + p + 1) * TT)
                if kb >= 2:
                    pe.wait_ge(t_moved, START + (CHUNKS + p) * KB + kb - 1)
                elif kb == 1:
                    pe.wait_ge(o_normed, normed)
                for t in range(TT):
                    last = nc.tensor.transpose(ps[:, 6 + kb % 2, bass.ts(t, P)], xn[:, t, bass.ts(kb, P)], ident[:, :])
                last.then_inc(t_ready, 1)

            def dense(p, t, half, kb, normed):
                if kb == 0:
                    pe.wait_ge(t_moved, START + (CHUNKS + p + 1) * KB)
                    if t:
                        pe.wait_ge(ffn_moved, START + (p * TT + t) * 2 - 1 + half)
                    if half:
                        pe.wait_ge(o_normed, normed)
                last = nc.tensor.matmul(ps[:, 6 + half, :], xn_t[:, kb, bass.ts(t, P)], w_eff[:, kb, bass.ts(half, N)],
                                        start=(kb == 0), stop=(kb == KB - 1))
                if kb == KB - 1:
                    last.then_inc(ffn_ready, 1)

            def attention(c, b, first):
                post = not first
                for g in range(G4):
                    pe.wait_ge(q_loaded[g % 2], (c * (G4 // 2) + g // 2 + 1) * 16 * PARTS)
                    for kt in range(KT):
                        for pair in range(2):
                            scores(c, b, g, kt, pair, first)
                        if kt == 0 and g:
                            values(c, b, g - 1, KT - 1)
                        elif kt:
                            if kt == 1 and not (first and g < 2):
                                pe.wait_ge(o_moved, c * G4 + g - 1)
                            values(c, b, g, kt - 1)
                        if kt == 2 and (g or post):
                            turn_o(c, g, post)
                        if post and g == 0 and kt == 5:
                            turn_back(c - 1)
                        if post and g == 0 and 8 <= kt < 8 + TT:
                            project(c - 1, kt - 8)
                        if post and g == 1 and 4 <= kt < 4 + KB:
                            turn_xn(c - 1, kt - 4, c * G4 + g)
                        if post and 2 <= g < 2 + TT:
                            dense(c - 1, g - 2, kt // KB, kt % KB, c * G4 + g)
                values(c, b, G4 - 1, KT - 1)

            attention(0, 0, True)
            with pe.Fori(1, CB) as c:
                attention(c, 0, False)
            with pe.Fori(CB, CHUNKS) as c:
                attention(c, 1, False)
            turn_o(CHUNKS, 0, True)
            turn_back(CHUNKS - 1)
            for t in range(TT):
                project(CHUNKS - 1, t)
            for kb in range(KB):
                turn_xn(CHUNKS - 1, kb, CHUNKS * G4)
            for t in range(TT):
                for half in range(2):
                    for kb in range(KB):
                        dense(CHUNKS - 1, t, half, kb, CHUNKS * G4)

        @block.vector
        def _(dve):
            class Chain:
                def __init__(self, s):
                    self.sem, self.n = s, 0

                def put(self, ins):
                    self.n += 1
                    ins.then_inc(self.sem, 1)

                def wait(self):
                    dve.wait_ge(self.sem, self.n)

                def then(self, ins):
                    self.put(ins)
                    self.wait()

                def end(self):
                    self.wait()
                    dve.sem_inc(self.sem, -self.n)

            def layernorm(tile):
                ch = Chain(v_ln)
                for t in range(TT):
                    for n in range(2):
                        ch.put(nc.vector.bn_stats(stats[:, t, n, :], tile(t)[:, bass.ts(n, N)]))
                ch.wait()
                for t in range(TT):
                    ch.put(nc.vector.bn_aggr(mv[:, t, :], stats[:, t, :, :].rearrange("p n s -> p (n s)")))
                ch.wait()
                v, r, a = nw[:, 0, :], nw[:, 3, :], nw[:, 1, :]
                ch.then(nc.vector.tensor_scalar(v, mv[:, :, 1], EPS, None, ALU.add))
                ch.then(nc.vector.tensor_scalar(a.bitcast(I32), v.bitcast(I32), 1, None, ALU.logical_shift_right))
                ch.then(nc.vector.tensor_scalar(r.bitcast(I32), a.bitcast(I32), -1.0, float(0x5F3759DF), ALU.mult, ALU.add))
                for _ in range(4):
                    ch.then(nc.vector.scalar_tensor_tensor(out=a, in0=r, scalar=-0.5, in1=r, op0=ALU.mult, op1=ALU.mult))
                    ch.then(nc.vector.tensor_tensor(a, a, v, ALU.mult))
                    ch.then(nc.vector.scalar_tensor_tensor(out=r, in0=a, scalar=1.5, in1=r, op0=ALU.add, op1=ALU.mult))
                ch.end()
                for t in range(TT):
                    nc.vector.tensor_scalar(xn[:, t, :], tile(t), mv[:, t, 0:1], r[:, t:t + 1], ALU.subtract, ALU.mult
                                            ).then_inc(xn_ready, 1)

            def split_shift(ch, done, more=None):
                ch.then(nc.vector.tensor_scalar(shift, ps[0:H, 6, :], -1.0, None, ALU.mult))
                if more:
                    more()
                ch.then(nc.vector.tensor_copy(q_parts[0:H, 0, :], shift))
                ch.then(nc.vector.tensor_tensor(shift_r, shift, q_parts[0:H, 0, :], ALU.subtract))
                ch.then(nc.vector.tensor_copy(q_parts[0:H, 1, :], shift_r))
                ch.end()
                nc.vector.tensor_tensor(q_parts[0:H, 2, :], shift_r, q_parts[0:H, 1, :], ALU.subtract).then_inc(done, 1)

            dve.wait_ge(const_ok, 4)
            ch = Chain(v_set)
            ch.put(nc.vector.memset(bias_row, 0.0))
            ch.put(nc.vector.tensor_copy(sel_latent[:, :].rearrange("p (h d) -> p h d", d=L),
                                         ident[:, 0:L].unsqueeze(1).to_broadcast([P, H, L])))
            ch.put(nc.vector.tensor_reduce(head_of_row[:, :], ident[:, :].rearrange("p (h d) -> p h d", d=L), AX.X, ALU.add))
            ch.wait()
            dve.wait_ge(w_in, W_IN)
            for j in range(PARTS):
                for i in range(PARTS):
                    col = 32 * j + W5 * i
                    ch.put(nc.vector.tensor_copy(w_down[:, :, col:col + L], wkv_in))
                    ch.put(nc.vector.tensor_copy(bias_row[:, col:col + L], bkv_row))
            for i in range(PARTS):
                ch.put(nc.vector.memset(bias_row[:, W5 * i + L:W5 * i + W5], 1.0))
            ch.put(nc.vector.tensor_copy(w_down[:, :, QROW:QROW + QL], wq_in))
            ch.put(nc.vector.tensor_copy(bias_row[:, QROW:QROW + QL], bq_row))
            ch.wait()
            ch.end()
            dve.sem_inc(down_ok, 1)
            dve.wait_ge(bias_ps, 1)
            nc.vector.tensor_copy(down_bias[:, :], ps[:, 7, 0:1]).then_inc(down_ok, 1)

            with dve.Fori(0, CHUNKS // 2) as i:
                for par in range(2):
                    c = i * 2 + par
                    dve.wait_ge(x_in[par], (i + 1) * TT * 16)
                    dve.wait_ge(t_ready, START + c * KB)
                    layernorm(lambda t: xt[:, par, t, :])
                    ch = Chain(v_lat)
                    cols = bass.ds(c * N, N)
                    dve.wait_ge(lat_ready, START + c + 1)
                    ch.put(nc.vector.tensor_copy(part_b[0:96, 0, :], lat[0:96, :]))
                    ch.put(nc.vector.tensor_copy(key_t[0:32, cols], lat[0:32, :]))
                    ch.put(nc.vector.tensor_reduce(c_max[:, bass.ds(c, 1)], lat[:, :], AX.X, ALU.max, apply_absolute_value=True))
                    ch.wait()
                    ch.then(nc.vector.tensor_tensor(part_f[0:96, 0, :], lat[0:96, :], part_b[0:96, 0, :], ALU.subtract))
                    ch.put(nc.vector.tensor_copy(key_t[32:64, cols], part_f[32:64, 0, :]))
                    ch.then(nc.vector.tensor_copy(part_b[64:96, 1, :], part_f[64:96, 0, :]))
                    nc.vector.tensor_tensor(key_t[64:96, cols], part_f[64:96, 0, :], part_b[64:96, 1, :], ALU.subtract
                                            ).then_inc(lat_split, 1)
                    dve.wait_ge(q_ps, START + c + 1)
                    dve.wait_ge(q_stored, START + c * PARTS * 16)
                    ch.put(nc.vector.tensor_scalar(q_parts[:, 0, :], ps[:, 5, :], bqk_sb[:, 0:1], SCALE, ALU.add, ALU.mult))
                    nc.vector.tensor_scalar(q_f32[:, cols], ps[:, 5, :], bqk_sb[:, 0:1], SCALE, ALU.add, ALU.mult
                                            ).then_inc(q_read, 1)
                    dve.wait_ge(q_read, START + c + 1)
                    ch.wait()
                    ch.then(nc.vector.tensor_tensor(part_f[:, 1, :], q_f32[:, cols], q_parts[:, 0, :], ALU.subtract))
                    ch.then(nc.vector.tensor_copy(q_parts[:, 1, :], part_f[:, 1, :]))
                    ch.end()
                    nc.vector.tensor_tensor(q_parts[:, 2, :], part_f[:, 1, :], q_parts[:, 1, :], ALU.subtract
                                            ).then_inc(q_split, 1)

            dve.wait_ge(q_stored, START + CHUNKS * PARTS * 16)
            for b in range(B):
                nc.vector.tensor_reduce(c_maxb[:, b:b + 1], c_max[:, bass.ts(b, CB)], AX.X, ALU.max).then_inc(bound_w_ready, 1)
                dve.wait_ge(bound_w_ps, b + 1)
                nc.vector.tensor_scalar(bound_w[:, b, :], head_of_row[:, :], ps[:, 7, b:b + 1], None, ALU.mult
                                        ).then_inc(bound_w_ready, 1)
                with dve.Fori(b * CB, (b + 1) * CB) as c:
                    ch = Chain(v_shift)
                    dve.wait_ge(bound_ps, START + c + 1)
                    dve.wait_ge(shift_stored, START + c * PARTS * 16)
                    split_shift(ch, shift_split, lambda: ch.then(
                        nc.vector.tensor_reduce(shift_min[:, bass.ds(c, 1)], shift, AX.X, ALU.min)))
            dve.wait_ge(shift_split, START + CHUNKS)
            nc.vector.tensor_reduce(shift_min[:, CHUNKS:CHUNKS + 1], shift_min[:, 0:CHUNKS], AX.X, ALU.min).then_inc(min_ready, 1)
            dve.wait_ge(tight_ps, 1)
            ch = Chain(v_set)
            ch.then(nc.vector.tensor_reduce(tight_f[:, 0:1], ps[0:1, 7, 0:H], AX.X, ALU.min))
            ch.end()
            nc.vector.tensor_scalar(tight[:, :], tight_f[:, 0:1], -BOUND_LIMIT, None, ALU.is_ge).then_inc(tight_ok, 1)
            dve.wait_ge(tight_ok, 1)
            with dve.If(dve.value_load(tight[:, :], min_val=0, max_val=1) < 1):
                dve.wait_ge(shift_stored, START + CHUNKS * PARTS * 16)
                with dve.Fori(0, CHUNKS) as c:
                    with dve.Fori(0, G4) as g:
                        for u in range(4 * TT):
                            dve.wait_ge(m_scores, u + 1)
                            nc.vector.tensor_reduce(row_max[:, u % TT, bass.ds(g * 4 + u // TT, 1)],
                                                    ps[:, 4 * (u % 2):4 * (u % 2) + KT // 4, :], AX.XY, ALU.max
                                                    ).then_inc(m_max, 1)
                        dve.sem_inc(m_scores, -4 * TT)
                    dve.wait_ge(m_sum_ps, 1)
                    dve.sem_inc(m_sum_ps, -1)
                    split_shift(Chain(v_shift), m_split)

            dve.wait_ge(prep_ps, 1)
            nc.vector.tensor_copy(wvbv_t, ps[:, 6, 0:G4 * L + G4]).then_inc(prep_ok, 1)
            dve.wait_ge(prep_ok, 1)
            ch = Chain(v_set)
            ch.put(nc.vector.memset(xt[:, 1, 0, :], 0.0))
            ch.wait()
            for g in range(G4):
                for h in range(4):
                    last = nc.vector.tensor_copy(lv[32 * h:32 * h + 32, g, 16 * g + L * h:16 * g + L * h + L],
                                                 wv_t[32 * h:32 * h + 32, g, :])
            last.then_inc(prep_ok, 1)
            for half in range(2):
                dve.wait_ge(prep_ps, 2 + half)
                nc.vector.tensor_scalar(lora_bt[:, bass.ts(half, N)], ps[:, 7 - half, :], coef, LORA_SCALE, ALU.mult, ALU.mult
                                        ).then_inc(prep_ok, 1)
            for g in range(G4):
                last = nc.vector.tensor_scalar(bv_wide[:, g, :], ones[:, :], bv_col[:, g:g + 1], None, ALU.mult)
            last.then_inc(prep_ok, 1)
            for n in range(2):
                dve.wait_ge(prep_ps, PREP_PS_LORA + n + 1)
                nc.vector.tensor_copy(w_vo[:, bass.ts(n, N)], ps[:, 6 + n, :]).then_inc(prep_ok, 1)
            for n in range(2):
                dve.wait_ge(prep_ps, PREP_PS_VO + n + 1)
                nc.vector.tensor_tensor(attn_bias[:, bass.ts(n, N)], ps[:, 6 + n, :], attn_bias[:, bass.ts(n, N)], ALU.add
                                        ).then_inc(prep_ok, 1)
            for half in range(2):
                for kb in range(KB):
                    dve.wait_ge(prep_ps, PREP_PS_BIAS + half * KB + kb + 1)
                    nc.vector.tensor_copy(w_eff[:, kb, bass.ts(half, N)], ps[:, 6 + kb % 2, :]).then_inc(prep_ok, 1)

            def move_o(c, g):
                dve.wait_ge(pv_done, (c * G4 + g) * KT)
                dve.wait_ge(o_turned, c * G4 + g - 1)
                nc.vector.tensor_copy(o_sb[:, :], ps[:, 4 + (g - 1) % 2, :]).then_inc(o_moved, 1)

            def norm_o(c, g):
                k = (g - 1) % G4
                dve.wait_ge(o_turned, c * G4 + g)
                dve.wait_ge(o_back, START + c if g else c - 1)
                turned = ps[:, 7, :].rearrange("p (t h m) -> p t h m", t=TT, h=4)
                nc.vector.reciprocal(recip[:, :, :], turned[:, :, :, L]).then_inc(v_rec, 1)
                dve.wait_ge(v_rec, c * G4 + g)
                nc.vector.tensor_tensor(o_q[:, :, 16 * k:16 * k + 16].rearrange("p t (h d) -> p t h d", d=L),
                                        turned[:, :, :, 0:L], recip[:, :, :].unsqueeze(3).to_broadcast([P, TT, 4, L]),
                                        ALU.mult).then_inc(o_normed, 1)

            def residual(p):
                dve.wait_ge(o_back, START + p + 1)
                dve.wait_ge(proj_ready, START + p * 2 * TT)
                nc.vector.tensor_copy(o_t[:, :], ps[:, 6, :]).then_inc(o_t_ready, 1)
                for t in range(TT):
                    dve.wait_ge(xb_ready, p * TT + t + 1)
                    for n in range(2):
                        dve.wait_ge(proj_ready, START + (p * TT + t) * 2 + n + 1)
                        nc.vector.tensor_tensor(y[:, t, bass.ts(n, N)], ps[:, 6 + n, :], y[:, t, bass.ts(n, N)], ALU.add
                                                ).then_inc(y_ready, 1)
                dve.wait_ge(y_ready, START + (p + 1) * 2 * TT)
                dve.wait_ge(t_ready, START + (CHUNKS + p) * KB)
                layernorm(lambda t: y[:, t, :])

            def move_xn(p):
                dve.wait_ge(ffn_ready, START + p * 2 * TT)
                for kb in range(KB):
                    dve.wait_ge(t_ready, START + (CHUNKS + p) * KB + kb + 1)
                    nc.vector.tensor_copy(xn_t[:, kb, :], ps[:, 6 + kb % 2, :]).then_inc(t_moved, 1)

            def add_dense(p, t):
                dve.wait_ge(yb_ready, p * TT + t + 1)
                for half in range(2):
                    dve.wait_ge(ffn_ready, START + (p * TT + t) * 2 + half + 1)
                    nc.vector.tensor_tensor(y[:, t, bass.ts(half, N)], ps[:, 6 + half, :], y[:, t, bass.ts(half, N)], ALU.add
                                            ).then_inc(ffn_moved, 1)

            def beside_attention(c, first):
                for g in range(G4):
                    if g or not first:
                        move_o(c, g)
                        norm_o(c, g)
                    if not first and g == 0:
                        residual(c - 1)
                    if not first and g == 1:
                        move_xn(c - 1)
                    if not first and 2 <= g < 2 + TT:
                        add_dense(c - 1, g - 2)

            beside_attention(0, True)
            with dve.Fori(1, CHUNKS) as c:
                beside_attention(c, False)
            move_o(CHUNKS, 0)
            norm_o(CHUNKS, 0)
            residual(CHUNKS - 1)
            move_xn(CHUNKS - 1)
            for t in range(TT):
                add_dense(CHUNKS - 1, t)


_INS = ["L0_attn_x", "L0_attn_Wq_d", "L0_attn_bq_d", "L0_attn_W_qk", "L0_attn_b_qk", "L0_attn_Wkv_d", "L0_attn_bkv_d",
        "L0_attn_Wv_u", "L0_attn_bv_u", "L0_attn_Wo", "L0_attn_bo", "L0_ffn_lora_A", "L0_ffn_lora_B", "L0_ffn_W",
        "L0_ffn_bias", "L0_ffn_lora_weights"]


def kernel(**inputs):
    import numpy as _np
    import concourse.bacc as _bacc
    from concourse import mybir as _mybir
    from concourse.bass_utils import run_bass_kernel_spmd as _run

    nc = _bacc.Bacc("TRN2", target_bir_lowering=False, num_devices=1)
    arrays, args = {}, []
    for name in _INS:
        a = _np.ascontiguousarray(inputs[name])
        arrays[f"in_{name}_dram"] = a
        args.append(nc.dram_tensor(f"in_{name}_dram", a.shape, _mybir.dt.from_np(a.dtype), kind="ExternalInput").ap())
    shape = inputs["L0_attn_x"].shape
    args.append(nc.dram_tensor("out_0_dram", shape, F32, kind="ExternalOutput").ap())
    build_block(nc, *args)
    r = _run(nc, [arrays], core_ids=[0])
    return r.results[0]["out_0_dram"]
```

```python
from contextlib import ExitStack

import concourse.bass as bass
from concourse import mybir

F32 = mybir.dt.float32
F32R = mybir.dt.float32r
BF16 = mybir.dt.bfloat16
I32 = mybir.dt.int32
ALU = mybir.AluOpType
ACT = mybir.ActivationFunctionType
AX = mybir.AxisListType

P = 128
N = 512


def build_block(nc, x, wq_d, bq_d, w_qk, b_qk, wkv_d, bkv_d, wv_u, bv_u, wo, bo,
                lora_a, lora_b, w_ffn, bias_ffn, lora_w, out):
    B, S, D = x.shape
    QL = wq_d.shape[1]
    L = wkv_d.shape[1]
    H = w_qk.shape[1] // L
    HD = wv_u.shape[1] // H
    NL, RANK = lora_a.shape[0], lora_a.shape[1]
    LORA_SCALE = 2.0
    EPS = 1e-5
    SCALE = L ** -0.5
    BOUND_LIMIT = 30.0
    T = B * S
    CHUNKS = T // N
    CB = S // N
    TT = N // P
    KT = S // P
    KB = D // P
    G4 = H // 4
    W5 = L + 1
    PARTS = 3
    ROWS = PARTS * W5
    QROW = 96
    assert H * L == P and NL * RANK == P and D == 2 * N and HD == 32

    x_t = x.rearrange("b s d -> (b s) d").rearrange("(t p) d -> t p d", p=P)
    out_t = out.rearrange("b s d -> (b s) d").rearrange("(t p) d -> t p d", p=P)
    qd = nc.dram_tensor("q_parts", [H, ROWS, T], BF16, kind="Internal").ap()

    with ExitStack() as ctx:
        def sb(name, shape, dt):
            return ctx.enter_context(nc.sbuf_tensor(name, shape, dt))

        def sem(name):
            return ctx.enter_context(nc.semaphore(name))

        ps = ctx.enter_context(nc.psum_tensor("ps", [P, 8, N], F32))

        ident = sb("ident", [P, P], F32)
        ones = sb("ones", [P, P], F32)
        head_of_row = sb("head_of_row", [P, H], F32)
        w_down = sb("w_down", [P, KB, 32], F32)
        fold = sb("fold", [P, 32], F32)
        spread = sb("spread", [P, P], F32)
        down_bias = sb("down_bias", [P, 1], F32)
        wqk_sb = sb("wqk_sb", [P, P], F32)
        bqk_sb = sb("bqk_sb", [P, 2], F32)
        sel_latent = sb("sel_latent", [P, P], F32)
        lora_a_sb = sb("lora_a_sb", [P, D], F32)
        lora_bt = sb("lora_bt", [P, D], F32)
        lv = sb("lv", [P, G4, 32], F32)
        bv_wide = sb("bv_wide", [P, G4, 32], F32)
        attn_bias = sb("attn_bias", [P, D], F32)
        ffn_bias = sb("ffn_bias", [P, D], F32)
        w_vo = sb("w_vo", [P, 2, D], F32R)
        o_t = sb("o_t", [P, 2, N], F32R)
        xn_t = sb("xn_t", [P, 2, 2, KB, P], F32R)
        AREA = 2 * KB * D
        area_at = nc.sbuf_base
        area = sb("area", [P, AREA], F32)
        w_eff = nc.alloc_sbuf_tensor_at("w_eff", [P, 2, KB, D], F32R, offset=area_at)
        q_f32 = area[:, 0:T]
        xn_b = area[:, T:T + TT * D].rearrange("p (t d) -> p t d", t=TT)
        xt_b = area[:, T + TT * D:T + 2 * TT * D].rearrange("p (t d) -> p t d", t=TT)
        x_turned = area[:, T + 2 * TT * D:T + 2 * TT * D + KB * N].rearrange("p (k n) -> p k n", k=KB)
        key_t = sb("key_t", [P, T], BF16)
        CW = 3 * W5
        c_wide = sb("c_wide", [P, T // P, CW + 32], F32)
        q_in = sb("q_in", [P, 2, 4, N], BF16)
        probs_at = nc.sbuf_base
        probs = sb("probs", [P, 2, 4 * N], F32)
        q_parts = nc.alloc_sbuf_tensor_at("q_parts_sb", [P, 2, PARTS, N], BF16, offset=probs_at)
        lat = nc.alloc_sbuf_tensor_at("lat", [P, 2, N], F32, offset=probs_at + 4 * PARTS * N)
        down_part = nc.alloc_sbuf_tensor_at("down_part", [P, N], F32, offset=probs_at + 4 * (PARTS + 2) * N)
        part_b = nc.alloc_sbuf_tensor_at("part_b", [P, 2, N], BF16, offset=probs_at + 4 * (PARTS + 3) * N)
        part_f = sb("part_f", [P, 2, N], F32)
        o_sb = sb("o_sb", [P, N], F32)
        o_q = sb("o_q", [P, TT, H * L], F32)
        recip = sb("recip", [P, TT, 4, 4], F32)
        y = sb("y", [P, TT, D], F32)
        xn = sb("xn", [P, TT, D], F32)
        stats = sb("stats", [P, TT, 2, 6], F32)
        mv = sb("mv", [P, TT, 2], F32)
        nw = sb("nw", [P, 4, TT], F32)
        c_max = sb("c_max", [P, CHUNKS], F32)
        c_maxb = sb("c_maxb", [P, B], F32)
        bound_w = sb("bound_w", [P, B, H], F32)
        small = sb("small", [P, 512], F32)
        shift_min = sb("shift_min", [P, B + 1], F32)
        tight_f = sb("tight_f", [1, 1], F32)
        tight = sb("tight", [1, 1], I32)
        row_max = sb("row_max", [P, TT, H], F32)

        x_tiles = [y, xt_b]
        xn_tiles = [xn, xn_b]
        q_abs = y[:, :, :].rearrange("p t (a n) -> p (t a) n", n=N)
        w_stage = [y, xn]
        lora_b_sb = xn_b[:, 0, :].rearrange("p (a n r) -> p a n r", a=KB, n=NL)
        wv_in = xn_b[0:L, 1, :]
        wkv_in = small[:, 0:KB * L].rearrange("p (k n) -> p k n", k=KB)
        wq_in = small[:, 32:32 + KB * QL].rearrange("p (k n) -> p k n", k=KB)
        coef = small[:, 136:137]
        wvbv_t = small[:, 144:144 + G4 * L + G4]
        wv_t = wvbv_t[:, 0:G4 * L].rearrange("p (g n) -> p g n", g=G4)
        bv_col = wvbv_t[:, G4 * L:G4 * L + G4]
        bias_row = small[0:1, 192:192 + P]
        bkv_row = small[0:1, 320:320 + L]
        bq_row = small[0:1, 330:330 + QL]
        bv_rows = small[0:G4, 384:384 + P]

        w_in = sem("w_in")
        lora_in = sem("lora_in")
        stage_in = [sem("stage_in0"), sem("stage_in1")]
        const_ok = sem("const_ok")
        pool_zero = sem("pool_zero")
        q_zero = sem("q_zero")
        bias_ps = sem("bias_ps")
        down_ok = sem("down_ok")
        v_set, v_ln, v_lat, v_shift, v_rec, v_hi = (sem(n) for n in ("v_set", "v_ln", "v_lat", "v_shift", "v_rec", "v_hi"))
        prep_ps = sem("prep_ps")
        prep_ok = sem("prep_ok")
        x_in = [[sem(f"x_in{half}_{t}") for t in range(TT)] for half in range(2)]
        xn_ready = sem("xn_ready")
        t_ready = sem("t_ready")
        t_moved = sem("t_moved")
        down_done = sem("down_done")
        part_ready = sem("part_ready")
        spread_ps = sem("spread_ps")
        lat_ready = sem("lat_ready")
        q_ps = sem("q_ps")
        caug_ps = sem("caug_ps")
        caug_ready = sem("caug_ready")
        lat_split = sem("lat_split")
        q_read = sem("q_read")
        q_split = sem("q_split")
        q_stored = [sem("q_stored0"), sem("q_stored1")]
        abs_ready = sem("abs_ready")
        bound_w_ps = sem("bound_w_ps")
        bound_w_ready = sem("bound_w_ready")
        bound_ps = sem("bound_ps")
        shift_split = sem("shift_split")
        shift_stored = sem("shift_stored")
        min_ready = sem("min_ready")
        tight_ps = sem("tight_ps")
        tight_ok = sem("tight_ok")
        m_loaded = sem("m_loaded")
        m_scores = sem("m_scores")
        m_max = sem("m_max")
        m_abs = sem("m_abs")
        m_used = sem("m_used")
        m_sum_ps = sem("m_sum_ps")
        m_split = sem("m_split")
        m_read = sem("m_read")
        m_stored = sem("m_stored")
        q_loaded = [sem("q_loaded0"), sem("q_loaded1")]
        s_ready = sem("s_ready")
        exp_done = sem("exp_done")
        pv_done = sem("pv_done")
        o_moved = sem("o_moved")
        o_turned = sem("o_turned")
        o_normed = sem("o_normed")
        o_back = sem("o_back")
        o_t_ready = sem("o_t_ready")
        proj_ready = sem("proj_ready")
        y_ready = sem("y_ready")
        ffn_ready = sem("ffn_ready")
        ffn_moved = sem("ffn_moved")
        x_back = sem("x_back")
        xb_ready = sem("xb_ready")
        yb_ready = sem("yb_ready")
        out_done = sem("out_done")

        block = ctx.enter_context(nc.Block())

        W_IN = 11 * 16
        PAIRS = 2 * KT
        UNITS = 2 * TT
        START = 2
        START_AT_2 = (t_moved, lat_ready, caug_ready, q_read, lat_split, caug_ps, q_ps, part_ready, spread_ps,
                      t_ready, ffn_moved, y_ready, proj_ready, o_back, ffn_ready)
        Q_STORES = 16 * PARTS
        SHIFTS = 16 * PARTS * CHUNKS
        PREP_LORA, PREP_VO, PREP_PART, PREP_BIAS, PREP_W = 2, 4, 6, 8, 10
        PREP_ALL = PREP_W + 2 * KB

        def prep_bank(m):
            return 6 + (m + 1) % 2

        @block.sync
        def _(sp):
            for s in START_AT_2:
                sp.sem_inc(s, START)
            for slot in range(2):
                sp.sem_inc(q_stored[slot], Q_STORES)
            for t in range(TT):
                sp.dma_start(y[:, t, :], x_t[t]).then_inc(x_in[0][t], 16)
            sp.dma_start(wkv_in, wkv_d.rearrange("(k p) n -> p k n", p=P)).then_inc(w_in, 16)
            sp.dma_start(wq_in, wq_d.rearrange("(k p) n -> p k n", p=P)).then_inc(w_in, 16)
            sp.dma_start(wqk_sb[QROW:QROW + QL, :], w_qk).then_inc(w_in, 16)
            sp.dma_start(bq_row, bq_d.rearrange("(a n) -> a n", a=1)).then_inc(w_in, 16)
            sp.dma_start(bkv_row, bkv_d.rearrange("(a n) -> a n", a=1)).then_inc(w_in, 16)
            sp.dma_start(bqk_sb[:, 0:1], b_qk.rearrange("(p a) -> p a", a=1)).then_inc(w_in, 16)
            sp.dma_start(bv_rows, bv_u.rearrange("(g p) -> g p", p=P)).then_inc(w_in, 16)
            sp.dma_start(coef, lora_w.rearrange("(n a b) -> n a b", a=1, b=1).to_broadcast([NL, RANK, 1])
                         ).then_inc(w_in, 16)
            for t in range(TT):
                sp.dma_start(xt_b[:, t, :], x_t[TT + t]).then_inc(x_in[1][t], 16)
            sp.dma_start(attn_bias[:, :], bo.rearrange("(a n) -> a n", a=1).to_broadcast([P, D])).then_inc(w_in, 16)
            sp.dma_start(ffn_bias[:, :], bias_ffn.rearrange("(a n) -> a n", a=1).to_broadcast([P, D])).then_inc(w_in, 16)
            sp.dma_start(lora_a_sb[:, :], lora_a.rearrange("n r d -> (n r) d")).then_inc(w_in, 16)

            def load_tiles(c, half):
                for t in range(TT):
                    sp.wait_ge(xn_ready, c * TT + t + 1)
                    sp.dma_start(x_tiles[half][:, t, :], x_t[(c + 2) * TT + t]).then_inc(x_in[half][t], 16)

            def store_q(c, slot):
                sp.wait_ge(q_split, c + 1)
                for k in range(PARTS):
                    sp.dma_start(qd[:, k * W5:k * W5 + L, bass.ds(c * N, N)], q_parts[:, slot, k, :]).then_inc(q_stored[slot], 16)

            for half in range(2):
                load_tiles(half, half)
            with sp.Fori(1, CHUNKS // 2 - 1) as i:
                for half in range(2):
                    load_tiles(i * 2 + half, half)
                    store_q(i * 2 + half - 2, half)
            for c in range(CHUNKS - 4, CHUNKS):
                store_q(c, c % 2)
            for b in range(B):
                sp.wait_ge(shift_split, b + 1)
                for j in range(CB):
                    for k in range(PARTS):
                        sp.dma_start(qd[:, k * W5 + L, (b * CB + j) * N:(b * CB + j + 1) * N],
                                     q_parts[32 * j:32 * j + H, b, k, :]).then_inc(shift_stored, 16)

            def load_q(c, g, slot, done):
                src = qd[bass.ds(g * 4, 4), :, bass.ds(c * N, N)].rearrange("h r n -> r h n")
                for j in range(PARTS):
                    sp.dma_start(q_in[32 * j:32 * j + ROWS, slot], src).then_inc(done, 16)

            for slot in range(2):
                sp.wait_ge(q_stored[slot], Q_STORES * (1 + CHUNKS // 2))
            sp.wait_ge(shift_stored, SHIFTS)
            sp.wait_ge(q_zero, 1)
            sp.wait_ge(tight_ok, 1)
            with sp.If(sp.value_load(tight[:, :], min_val=0, max_val=1) < 1):
                with sp.Fori(0, CHUNKS) as c:
                    with sp.Fori(0, G4) as g:
                        load_q(c, g, 0, m_loaded)
                        sp.wait_ge(m_read, 1)
                        sp.sem_inc(m_read, -1)
                    sp.wait_ge(m_split, c + 1)
                    for k in range(PARTS):
                        sp.dma_start(qd[:, k * W5 + L, bass.ds(c * N, N)], q_parts[0:H, 0, k, :]).then_inc(m_stored, 16)
                    sp.wait_ge(m_stored, PARTS * 16)
                    sp.sem_inc(m_stored, -PARTS * 16)

            load_q(0, 0, 0, q_loaded[0])
            sp.wait_ge(bound_ps, B)
            sp.wait_ge(t_ready, START + CHUNKS * KB)
            sp.dma_start(wv_in, wv_u).then_inc(lora_in, 16)
            for a in range(KB):
                sp.dma_start(lora_b_sb[:, a], lora_b[:, a * P:(a + 1) * P, :].rearrange("n o r -> o n r")
                             ).then_inc(lora_in, 16)
            for half in range(2):
                sp.dma_start(w_stage[half][:, :, :].rearrange("p t (a n) -> p (t a) n", n=N),
                             wo[:, half * N:(half + 1) * N].rearrange("(a p) n -> p a n", p=P)).then_inc(stage_in[half], 16)

            def load_w():
                for half in range(2):
                    sp.wait_ge(prep_ps, PREP_PART + half)
                    sp.dma_start(w_stage[half][:, :, :], w_ffn[half * 4 * P:(half + 1) * 4 * P, :]
                                 .rearrange("(a p) n -> p a n", p=P)).then_inc(stage_in[half], 16)

            def load_x(c, first):
                if first:
                    sp.wait_ge(prep_ps, PREP_W + KB - 1)
                else:
                    sp.wait_ge(out_done, c * TT * 16)
                for t in range(TT):
                    sp.dma_start(y[:, t, :], x_t[c * TT + t]).then_inc(x_back, 16)

            def store_out(p, t):
                sp.wait_ge(ffn_moved, START + (p * TT + t + 1) * 2)
                sp.dma_start(out_t[p * TT + t], y[:, t, :]).then_inc(out_done, 16)

            def beside_attention(c, first, last):
                for g in range(G4):
                    if not (first and g == 0):
                        sp.wait_ge(s_ready, PAIRS * (c * G4 + g))
                    if g < G4 - 1:
                        load_q(c, g + 1, (g + 1) % 2, q_loaded[(g + 1) % 2])
                    elif not last:
                        load_q(c + 1, 0, 0, q_loaded[0])
                    if first and g == 2:
                        load_w()
                    if not first and 3 <= g < 3 + TT:
                        store_out(c - 1, g - 3)
                load_x(c, first)

            beside_attention(0, True, False)
            with sp.Fori(1, CHUNKS - 1) as c:
                beside_attention(c, False, False)
            beside_attention(CHUNKS - 1, False, True)
            for t in range(TT):
                store_out(CHUNKS - 1, t)
            sp.wait_ge(out_done, CHUNKS * TT * 16)

        @block.gpsimd
        def _(pool):
            pool.memset(ident[:, :], 0.0).then_inc(pool_zero, 1)
            pool.wait_ge(pool_zero, 1)
            pool.affine_select(out=ident[:, :], in_=ident[:, :], compare_op=ALU.not_equal, fill=1.0, base=0,
                               pattern=[[-1, P]], channel_multiplier=1).then_inc(const_ok, 1)
            pool.memset(ones[:, :], 1.0).then_inc(const_ok, 1)
            pool.memset(w_down[:, :, :], 0.0).then_inc(const_ok, 1)
            pool.memset(spread[:, :], 0.0).then_inc(const_ok, 1)
            pool.memset(key_t[:, :], 0.0).then_inc(const_ok, 1)
            pool.memset(c_wide[:, :, :], 0.0).then_inc(const_ok, 1)
            pool.memset(q_in[:, :, :, :], 0.0).then_inc(q_zero, 1)
            pool.wait_ge(prep_ok, PREP_W)
            with pool.Fori(0, CHUNKS) as c:
                pool.wait_ge(x_back, (c + 1) * TT * 16)
                for t in range(TT):
                    pool.tensor_tensor(y[:, t, :], y[:, t, :], attn_bias[:, :], ALU.add).then_inc(xb_ready, 1)
                for t in range(TT):
                    pool.wait_ge(xn_ready, (CHUNKS + c) * TT + t + 1)
                    pool.tensor_tensor(y[:, t, :], y[:, t, :], ffn_bias[:, :], ALU.add).then_inc(yb_ready, 1)

        @block.scalar
        def _(act):
            act.sem_inc(down_done, KB)
            act.wait_ge(down_ok, 3)

            def move_turned(c, kb):
                act.wait_ge(t_ready, START + c * KB + kb + 1)
                act.wait_ge(down_done, c * KB + kb + 1)
                nc.scalar.activation(x_turned[:, kb, :], ps[:, kb % 4, :], ACT.Copy).then_inc(t_moved, 1)

            def move_latents(c, slot):
                act.wait_ge(lat_split, START + c - 1)
                act.wait_ge(spread_ps, START + c + 1)
                nc.scalar.activation(lat[:, slot, :], ps[:, 5, :], ACT.Identity, bias=down_bias[:, 0:1]
                                     ).then_inc(lat_ready, 1)

            def move_products(c, slot, rounds):
                act.wait_ge(caug_ps, START + c + 1)
                nc.scalar.activation(c_wide[:, bass.ds(c * TT, TT), CW:CW + W5],
                                     ps[:, 6, :].rearrange("p (t m) -> p t m", t=TT)[:, :, 0:W5], ACT.Copy
                                     ).then_inc(caug_ready, 1)
                act.wait_ge(q_stored[slot], Q_STORES * (rounds + 1))
                act.wait_ge(q_ps, START + c + 1)
                nc.scalar.activation(q_parts[:, slot, 0, :], ps[:, 7, :], ACT.Identity, bias=bqk_sb[:, 1:2], scale=SCALE
                                     ).then_inc(q_read, 1)
                nc.scalar.activation(q_f32[:, bass.ds(c * N, N)], ps[:, 7, :], ACT.Identity, bias=bqk_sb[:, 1:2], scale=SCALE
                                     ).then_inc(q_read, 1)

            def move_chunk(c, slot, rounds, first=False):
                for kb in range(KB):
                    move_turned(c, kb)
                    if kb == 1 and not first:
                        move_latents(c - 1, 1 - slot)
                    if kb == 4 and not first:
                        move_products(c - 1, 1 - slot, rounds)
                act.wait_ge(spread_ps, START + c)
                act.wait_ge(down_done, (c + 2) * KB)
                nc.scalar.activation(down_part[:, :], ps[:, 4, :], ACT.Copy).then_inc(part_ready, 1)

            move_chunk(0, 0, 0, True)
            with act.Fori(0, CHUNKS // 2 - 1) as i:
                for half in range(2):
                    move_chunk(i * 2 + half + 1, 1 - half, i)
            move_chunk(CHUNKS - 1, 1, CHUNKS // 2 - 1)
            move_latents(CHUNKS - 1, 1)
            move_products(CHUNKS - 1, 1, CHUNKS // 2 - 1)
            act.wait_ge(q_read, START + 2 * CHUNKS)
            act.wait_ge(xn_ready, (CHUNKS - 1) * TT)
            for b in range(B):
                nc.scalar.activation(q_abs[:, b * CB:(b + 1) * CB, :].rearrange("p a n -> p (a n)"),
                                     q_f32[:, b * S:(b + 1) * S], ACT.Abs).then_inc(abs_ready, 1)
            act.wait_ge(tight_ok, 1)
            with act.If(act.value_load(tight[:, :], min_val=0, max_val=1) < 1):
                with act.Fori(0, CHUNKS) as c:
                    nc.scalar.activation(lat[:, 0, :], q_f32[:, bass.ds(c * N, N)], ACT.Abs).then_inc(m_abs, 1)
                    act.wait_ge(m_used, 1)
                    act.sem_inc(m_used, -1)

            def exps(c, first):
                for g in range(G4):
                    for kt in range(KT):
                        for pair in range(2):
                            act.wait_ge(s_ready, (c * G4 + g) * PAIRS + 2 * kt + pair + 1)
                            if pair == 0 and not (first and g == 0 and kt < 2):
                                act.wait_ge(pv_done, (c * G4 + g) * KT + kt - 1)
                            nc.scalar.activation(probs[:, kt % 2, bass.ts(pair, 2 * N)],
                                                 ps[:, 2 * pair:2 * pair + 2, :].rearrange("p a n -> p (a n)"),
                                                 ACT.Exp).then_inc(exp_done, 1)

            exps(0, True)
            with act.Fori(1, CHUNKS) as c:
                exps(c, False)

        @block.tensor
        def _(pe):
            pe.wait_ge(w_in, W_IN)
            pe.wait_ge(const_ok, 6)
            pe.wait_ge(down_ok, 1)
            nc.tensor.matmul(ps[:, 7, 0:1], bias_row, ones[0:1, 0:1], start=True, stop=True).then_inc(bias_ps, 1)
            pe.wait_ge(down_ok, 2)

            def turn_x(c, slot, kb):
                if kb >= 4:
                    pe.wait_ge(t_moved, START + c * KB + kb - 3)
                for t in range(TT):
                    last = nc.tensor.transpose(ps[:, kb % 4, bass.ts(t, P)], xn_tiles[slot][:, t, bass.ts(kb, P)], ident[:, :])
                last.then_inc(t_ready, 1)

            def down(c, k):
                pe.wait_ge(t_moved, START + c * KB + k + 1)
                if k == 0:
                    pe.wait_ge(part_ready, START + c)
                i = k % 4
                nc.tensor.matmul(ps[32 * i:32 * i + 32, 4, :], w_down[:, k, :], x_turned[:, k, :], start=(k < 4), stop=(k >= 4)
                                 ).then_inc(down_done, 1)

            def sum_parts(c):
                pe.wait_ge(part_ready, START + c + 1)
                pe.wait_ge(lat_ready, START + c)
                nc.tensor.matmul(ps[:, 5, :], spread[:, :], down_part[:, :], start=True, stop=True).then_inc(spread_ps, 1)

            def use_latents(c, slot):
                pe.wait_ge(lat_ready, START + c + 1)
                pe.wait_ge(caug_ready, START + c)
                for t in range(TT):
                    last = nc.tensor.transpose(ps[:, 6, bass.ts(t, P)], lat[:, slot, bass.ts(t, P)], ident[:, :])
                last.then_inc(caug_ps, 1)
                pe.wait_ge(q_read, START + 2 * c)
                nc.tensor.matmul(ps[:, 7, :], wqk_sb[QROW:QROW + QL, :], lat[QROW:QROW + QL, slot, :], start=True, stop=True
                                 ).then_inc(q_ps, 1)

            def stage1(c, slot, first):
                pe.wait_ge(xn_ready, (c + 1) * TT)
                for kb in range(KB + 2):
                    if kb < KB:
                        turn_x(c, slot, kb)
                    if kb == 1 and not first:
                        sum_parts(c - 1)
                    if kb == 4 and not first:
                        use_latents(c - 1, 1 - slot)
                    if kb >= 2:
                        down(c, kb - 2)

            stage1(0, 0, True)
            with pe.Fori(0, CHUNKS // 2 - 1) as i:
                for half in range(2):
                    stage1(i * 2 + half + 1, 1 - half, False)
            stage1(CHUNKS - 1, 1, False)
            sum_parts(CHUNKS - 1)
            use_latents(CHUNKS - 1, 1)

            pe.wait_ge(bound_w_ready, 1)
            pe.wait_ge(q_read, START + 2 * CHUNKS)
            nc.tensor.matmul(ps[:, 7, 0:B], sel_latent[:, :], c_maxb[:, :], start=True, stop=True).then_inc(bound_w_ps, 1)
            for b in range(B):
                pe.wait_ge(bound_w_ready, 2 + b)
                pe.wait_ge(abs_ready, b + 1)
                for j in range(CB):
                    last = nc.tensor.matmul(ps[32 * j:32 * j + H, b, :], bound_w[:, b, :], q_abs[:, b * CB + j, :],
                                            start=True, stop=True)
                last.then_inc(bound_ps, 1)
            pe.wait_ge(min_ready, 1)
            nc.tensor.matmul(ps[0:1, 7, 0:P], shift_min[:, B:B + 1], ident[:, :], start=True, stop=True).then_inc(tight_ps, 1)
            pe.wait_ge(tight_ok, 1)
            with pe.If(pe.value_load(tight[:, :], min_val=0, max_val=1) < 1):
                for b in range(B):
                    with pe.Fori(b * CB, (b + 1) * CB) as c:
                        with pe.Fori(0, G4):
                            pe.wait_ge(m_loaded, PARTS * 16)
                            pe.sem_inc(m_loaded, -PARTS * 16)
                            for u in range(4 * TT):
                                if u >= 2:
                                    pe.wait_ge(m_max, u - 1)
                                for n in range(KT // 4):
                                    last = nc.tensor.matmul(ps[:, 4 * (u % 2) + n, :],
                                                            q_in[:, 0, u // TT, bass.ts(u % TT, P)],
                                                            key_t[:, b * S + n * N:b * S + (n + 1) * N], start=True, stop=True)
                                last.then_inc(m_scores, 1)
                            pe.wait_ge(m_max, 4 * TT)
                            pe.sem_inc(m_max, -4 * TT)
                            pe.drain().then_inc(m_read, 1)
                        pe.wait_ge(m_abs, 1)
                        pe.sem_inc(m_abs, -1)
                        nc.tensor.matmul(ps[0:H, 6, :], bound_w[:, b, :], lat[:, 0, :], start=True, stop=False).then_inc(m_used, 1)
                        for t in range(TT):
                            last = nc.tensor.matmul(ps[0:H, 6, bass.ts(t, P)], row_max[:, t, :], ident[:, :],
                                                    start=False, stop=(t == TT - 1))
                        last.then_inc(m_sum_ps, 1)
                        pe.wait_ge(m_split, c + 1)
            def free_bank(m):
                pe.wait_ge(prep_ok, m - 1)

            def turn_values():
                pe.wait_ge(lora_in, (KB + 1) * 16)
                for g in range(G4):
                    nc.tensor.transpose(ps[:, prep_bank(1), bass.ts(g, L)], wv_in[:, bass.ts(g, P)], ident[0:L, 0:L])
                nc.tensor.transpose(ps[:, prep_bank(1), G4 * L:G4 * L + G4], bv_rows, ident[0:G4, 0:G4]).then_inc(prep_ps, 1)

            def turn_lora(m):
                if m == PREP_LORA + 1:
                    free_bank(m)
                for a in range(4):
                    last = nc.tensor.transpose(ps[:, prep_bank(m), bass.ts(a, P)],
                                               lora_b_sb[:, (m - PREP_LORA) * 4 + a].rearrange("p n r -> p (n r)"), ident[:, :])
                last.then_inc(prep_ps, 1)

            def times_wo(m, weights, odd):
                half = m % 2
                if odd == 0:
                    free_bank(m)
                    pe.wait_ge(stage_in[half], 16)
                for g in range(odd, G4, 2):
                    i = g // 2
                    last = nc.tensor.matmul(ps[32 * i:32 * i + 32, prep_bank(m), :], weights[:, g, :],
                                            w_stage[half][:, g // 2, bass.ts(g % 2, N)], start=(odd == 0), stop=(odd == 1))
                if odd == 1:
                    last.then_inc(prep_ps, 1)

            def sum_bias(m):
                free_bank(m)
                nc.tensor.matmul(ps[:, prep_bank(m), :], ones[:, :], part_f[:, m % 2, :], start=True, stop=True
                                 ).then_inc(prep_ps, 1)

            def turn_w(k):
                m, kb, half = PREP_W + k, k % KB, k // KB
                free_bank(m)
                pe.wait_ge(stage_in[half], 32)
                if k == 4:
                    pe.wait_ge(o_normed, 1)
                for a in range(4):
                    nc.tensor.matmul(ps[:, prep_bank(m), bass.ts(a, P)], w_stage[half][:, a, bass.ts(kb, P)], ident[:, :],
                                     start=(a == 0), stop=False)
                nc.tensor.matmul(ps[:, prep_bank(m), :], lora_a_sb[:, bass.ts(kb, P)], lora_bt[:, bass.ts(half, N)],
                                 start=False, stop=True).then_inc(prep_ps, 1)

            def prepare(g, kt):
                if g == 0 and kt == 3:
                    turn_values()
                if g == 0 and kt in (6, 9):
                    turn_lora(PREP_LORA + kt // 9)
                if g == 1 and kt % 2 == 0:
                    times_wo(PREP_VO + kt // 4, lv if kt < 8 else bv_wide, kt // 2 % 2)
                if g == 2 and kt in (4, 8):
                    sum_bias(PREP_BIAS + kt // 8)
                if 3 <= g < 7 and kt in (4, 7, 10, 13):
                    turn_w((g - 3) * 4 + (kt - 4) // 3)

            def scores(c, b, g, kt, pair, first):
                if not (first and g == 0 and kt == 0):
                    pe.wait_ge(exp_done, (c * G4 + g) * PAIRS + 2 * kt + pair - 1)
                for h in (2 * pair, 2 * pair + 1):
                    last = nc.tensor.matmul(ps[:, h, :], key_t[:, bass.ts(b * KT + kt, P)], q_in[:, g % 2, h, :],
                                            start=True, stop=True)
                last.then_inc(s_ready, 1)

            def values(c, b, g, kt):
                at = CW - W5 * (g % 4)
                pe.wait_ge(exp_done, (c * G4 + g) * PAIRS + 2 * kt + 2)
                for h in range(4):
                    last = nc.tensor.matmul(ps[32 * h:32 * h + 32, 4 + g // 4, :], c_wide[:, b * KT + kt, at:at + 32],
                                            probs[:, kt % 2, bass.ts(h, N)], start=(kt == 0 and g % 4 == 0),
                                            stop=(kt == KT - 1 and g % 4 == 3))
                last.then_inc(pv_done, 1)

            def turn_o(c, half):
                pe.wait_ge(o_moved, 2 * c + half + 1)
                for t in range(TT):
                    last = nc.tensor.transpose(ps[:, 7, bass.ts(t, P)], o_sb[:, bass.ts(t, P)], ident[:, :])
                last.then_inc(o_turned, 1)

            THREE = ((0, 0), (0, 1), (1, 0))

            def turn_back(p):
                pe.wait_ge(o_normed, (p + 1) * 2)
                for t in range(TT):
                    last = nc.tensor.transpose(ps[:, 6, bass.ts(t, P)], o_q[:, t, :], ident[:, :])
                last.then_inc(o_back, 1)

            def project(p, t, banks):
                if t == 0:
                    pe.wait_ge(o_t_ready, p + 1)
                else:
                    pe.wait_ge(y_ready, START + (p * TT + t - (banks == 0)) * 2)
                at = 6 if banks else 2 * (t % 2)
                for n in range(2):
                    for i, (a, b) in enumerate(THREE):
                        last = nc.tensor.matmul(ps[:, at + n, :], o_t[:, a, bass.ts(t, P)], w_vo[:, b, bass.ts(n, N)],
                                                start=(i == 0), stop=(i == 2))
                    last.then_inc(proj_ready, 1)

            def turn_xn(p, t, u, bank):
                pe.wait_ge(xn_ready, (CHUNKS + p) * TT + t + 1)
                for a in range(4):
                    last = nc.tensor.transpose(ps[:, bank, bass.ts(a, P)], xn[:, t, bass.ts(4 * u + a, P)], ident[:, :])
                last.then_inc(t_ready, 1)

            def dense(p, t, half, kb):
                for i, (a, b) in enumerate(THREE):
                    last = nc.tensor.matmul(ps[:, 6 + half, :], xn_t[:, t % 2, a, kb, :], w_eff[:, b, kb, bass.ts(half, N)],
                                            start=(kb + i == 0), stop=(kb == KB - 1 and i == 2))
                if kb == KB - 1:
                    last.then_inc(ffn_ready, 1)

            def dense_beside(c, g, kt):
                p = c - 1
                if g == 0 and kt == 5:
                    pe.wait_ge(ffn_moved, START + p * 2 * TT)
                    turn_back(p)
                if g == 0 and 8 <= kt < 8 + TT:
                    project(p, kt - 8, 1)
                t = g - 1
                if 0 <= t < TT and kt == 4:
                    pe.wait_ge(ffn_moved, START + (p * TT + max(t - 1, 0)) * 2)
                    if g == 4:
                        pe.wait_ge(o_normed, 2 * c + 1)
                    turn_xn(p, t, 0, 7)
                if 0 <= t < TT and kt == 6:
                    pe.wait_ge(t_moved, START + CHUNKS * KB + (p * TT + t) * 2 + 1)
                    turn_xn(p, t, 1, 7)
                t = g - 2
                if 0 <= t < TT:
                    if kt == 0:
                        pe.wait_ge(t_moved, START + CHUNKS * KB + (p * TT + t + 1) * 2)
                        pe.wait_ge(ffn_moved, START + (p * TT + t) * 2 - 1)
                    if kt == KB:
                        if t < TT - 1:
                            pe.wait_ge(t_moved, START + CHUNKS * KB + (p * TT + t + 2) * 2)
                        pe.wait_ge(ffn_moved, START + (p * TT + t) * 2)
                    dense(p, t, kt // KB, kt % KB)

            def attention(c, b, first):
                for g in range(G4):
                    pe.wait_ge(q_loaded[g % 2], (c * (G4 // 2) + g // 2 + 1) * 16 * PARTS)
                    for kt in range(KT):
                        for pair in range(2):
                            scores(c, b, g, kt, pair, first)
                        if kt == 0 and g:
                            values(c, b, g - 1, KT - 1)
                        elif kt:
                            if kt == 1 and g % 4 == 0 and not first:
                                pe.wait_ge(o_moved, 2 * c - 1 + g // 4)
                            values(c, b, g, kt - 1)
                        if kt == 2 and g == 0 and not first:
                            pe.wait_ge(ffn_moved, START + (c - 1) * TT * 2)
                            turn_o(c - 1, 1)
                        if kt == 2 and g == 4:
                            if first:
                                pe.wait_ge(prep_ok, PREP_W + 4)
                            else:
                                pe.wait_ge(ffn_moved, START + ((c - 1) * TT + 2) * 2)
                            turn_o(c, 0)
                        if first:
                            prepare(g, kt)
                        else:
                            dense_beside(c, g, kt)
                values(c, b, G4 - 1, KT - 1)

            attention(0, 0, True)
            pe.wait_ge(prep_ok, PREP_ALL)
            with pe.Fori(1, CB) as c:
                attention(c, 0, False)
            with pe.Fori(CB, CHUNKS) as c:
                attention(c, 1, False)
            p = CHUNKS - 1
            turn_o(p, 1)
            turn_back(p)
            pe.wait_ge(exp_done, CHUNKS * G4 * PAIRS)
            for t in range(TT):
                project(p, t, 0)

            def turn_last(t):
                for u in range(2):
                    if t:
                        pe.wait_ge(t_moved, START + CHUNKS * KB + (p * TT + t - 1) * 2 + u + 1)
                    turn_xn(p, t, u, 4 + u)

            turn_last(0)
            for t in range(TT):
                if t < TT - 1:
                    turn_last(t + 1)
                for half in range(2):
                    pe.wait_ge(t_moved, START + CHUNKS * KB + (p * TT + t + 1) * 2)
                    if t:
                        pe.wait_ge(ffn_moved, START + (p * TT + t) * 2 - 1 + half)
                    for kb in range(KB):
                        dense(p, t, half, kb)

        @block.vector
        def _(dve):
            class Chain:
                def __init__(self, s):
                    self.sem, self.n = s, 0

                def put(self, ins):
                    self.n += 1
                    ins.then_inc(self.sem, 1)

                def wait(self):
                    dve.wait_ge(self.sem, self.n)

                def then(self, ins):
                    self.put(ins)
                    self.wait()

                def end(self):
                    self.wait()
                    dve.sem_inc(self.sem, -self.n)

            def layernorm(tile, out, arrived=None, tiles=range(TT)):
                ch = Chain(v_ln)
                for t in tiles:
                    if arrived:
                        arrived(t)
                    for n in range(2):
                        ch.put(nc.vector.bn_stats(stats[:, t, n, :], tile[:, t, bass.ts(n, N)]))
                ch.wait()
                for t in tiles:
                    ch.put(nc.vector.bn_aggr(mv[:, t, :], stats[:, t, :, :].rearrange("p n s -> p (n s)")))
                ch.wait()
                lo, hi = tiles[0], tiles[-1] + 1
                v, r, a = nw[:, 0, lo:hi], nw[:, 3, lo:hi], nw[:, 1, lo:hi]
                ch.then(nc.vector.tensor_scalar(v, mv[:, lo:hi, 1], EPS, None, ALU.add))
                ch.then(nc.vector.tensor_scalar(a.bitcast(I32), v.bitcast(I32), 1, None, ALU.logical_shift_right))
                ch.then(nc.vector.tensor_scalar(r.bitcast(I32), a.bitcast(I32), -1.0, float(0x5F3759DF), ALU.mult, ALU.add))
                for _ in range(3):
                    ch.then(nc.vector.scalar_tensor_tensor(out=a, in0=r, scalar=-0.5, in1=r, op0=ALU.mult, op1=ALU.mult))
                    ch.then(nc.vector.tensor_tensor(a, a, v, ALU.mult))
                    ch.then(nc.vector.scalar_tensor_tensor(out=r, in0=a, scalar=1.5, in1=r, op0=ALU.add, op1=ALU.mult))
                ch.end()
                for t in tiles:
                    nc.vector.tensor_scalar(out[:, t, :], tile[:, t, :], mv[:, t, 0:1], nw[:, 3, t:t + 1],
                                            ALU.subtract, ALU.mult).then_inc(xn_ready, 1)

            def split_shift(rows, bank, slot, done, smallest=None):
                ch = Chain(v_shift)
                shift, shift_r = part_f[0:rows, 0, :], part_f[0:rows, 1, :]
                parts = q_parts[0:rows, slot]
                ch.then(nc.vector.tensor_scalar(shift, ps[0:rows, bank, :], -1.0, None, ALU.mult))
                if smallest is not None:
                    ch.put(nc.vector.tensor_reduce(smallest, shift, AX.X, ALU.min))
                ch.then(nc.vector.tensor_copy(parts[:, 0, :], shift))
                ch.then(nc.vector.tensor_tensor(shift_r, shift, parts[:, 0, :], ALU.subtract))
                ch.then(nc.vector.tensor_copy(parts[:, 1, :], shift_r))
                ch.end()
                nc.vector.tensor_tensor(parts[:, 2, :], shift_r, parts[:, 1, :], ALU.subtract).then_inc(done, 1)

            def split_three_pass(high, low, bank_part, moved):
                ch = Chain(v_hi)
                ch.then(nc.vector.tensor_copy(high, bank_part))
                ch.end()
                nc.vector.tensor_tensor(low, bank_part, high.bitcast(F32), ALU.subtract).then_inc(moved, 1)

            dve.wait_ge(const_ok, 6)
            ch = Chain(v_set)
            ch.put(nc.vector.memset(bias_row, 0.0))
            ch.put(nc.vector.tensor_copy(sel_latent[:, :].rearrange("p (h d) -> p h d", d=L),
                                         ident[:, 0:L].unsqueeze(1).to_broadcast([P, H, L])))
            ch.put(nc.vector.tensor_reduce(head_of_row[:, :], ident[:, :].rearrange("p (h d) -> p h d", d=L), AX.X, ALU.add))
            ch.put(nc.vector.tensor_reduce(fold[:, :], ident[:, :].rearrange("p (i m) -> p m i", m=32), AX.X, ALU.add))
            ch.wait()
            for j in range(PARTS):
                ch.put(nc.vector.tensor_copy(spread[:, 32 * j:32 * j + 16], fold[:, 0:16]))
            ch.put(nc.vector.tensor_copy(spread[:, QROW:QROW + QL], fold[:, 16:16 + QL]))
            dve.wait_ge(w_in, W_IN)
            ch.put(nc.vector.tensor_scalar(bqk_sb[:, 1:2], bqk_sb[:, 0:1], SCALE, None, ALU.mult))
            for i in range(PARTS):
                ch.put(nc.vector.tensor_copy(w_down[:, :, W5 * i:W5 * i + L], wkv_in))
                for j in range(PARTS):
                    col = 32 * j + W5 * i
                    ch.put(nc.vector.tensor_copy(bias_row[:, col:col + L], bkv_row))
                ch.put(nc.vector.memset(bias_row[:, W5 * i + L:W5 * i + W5], 1.0))
            ch.put(nc.vector.tensor_copy(w_down[:, :, 16:16 + QL], wq_in))
            ch.put(nc.vector.tensor_copy(bias_row[:, QROW:QROW + QL], bq_row))
            ch.wait()
            ch.end()
            dve.sem_inc(down_ok, 1)
            dve.wait_ge(bias_ps, 1)
            nc.vector.tensor_copy(down_bias[:, :], ps[:, 7, 0:1]).then_inc(down_ok, 1)
            dve.sem_inc(down_ok, 1)

            def normalise(rounds, half):
                layernorm(x_tiles[half], xn_tiles[half], lambda t: dve.wait_ge(x_in[half][t], rounds * 16))

            def split_latents(c, slot):
                ch = Chain(v_lat)
                cols = bass.ds(c * N, N)
                src = lat[:, slot, :]
                dve.wait_ge(lat_ready, START + c + 1)
                ch.put(nc.vector.tensor_copy(part_b[0:96, 0, :], src[0:96, :]))
                ch.put(nc.vector.tensor_copy(key_t[0:32, cols], src[0:32, :]))
                ch.put(nc.vector.tensor_reduce(c_max[:, bass.ds(c, 1)], src, AX.X, ALU.max, apply_absolute_value=True))
                ch.wait()
                ch.then(nc.vector.tensor_tensor(part_f[0:96, 0, :], src[0:96, :], part_b[0:96, 0, :], ALU.subtract))
                ch.put(nc.vector.tensor_copy(key_t[32:64, cols], part_f[32:64, 0, :]))
                ch.then(nc.vector.tensor_copy(part_b[64:96, 1, :], part_f[64:96, 0, :]))
                nc.vector.tensor_tensor(key_t[64:96, cols], part_f[64:96, 0, :], part_b[64:96, 1, :], ALU.subtract
                                        ).then_inc(lat_split, 1)
                dve.wait_ge(q_read, START + 2 * c + 2)
                ch.then(nc.vector.tensor_tensor(part_f[:, 1, :], q_f32[:, cols], q_parts[:, slot, 0, :], ALU.subtract))
                ch.then(nc.vector.tensor_copy(q_parts[:, slot, 1, :], part_f[:, 1, :]))
                ch.end()
                nc.vector.tensor_tensor(q_parts[:, slot, 2, :], part_f[:, 1, :], q_parts[:, slot, 1, :], ALU.subtract
                                        ).then_inc(q_split, 1)

            for half in range(2):
                normalise(1, half)
            with dve.Fori(1, CHUNKS // 2) as i:
                for half in range(2):
                    dve.wait_ge(t_ready, START + (i * 2 + half - 1) * KB)
                    normalise(i + 1, half)
                    split_latents(i * 2 + half - 2, half)
            for c in range(CHUNKS - 2, CHUNKS):
                split_latents(c, c % 2)

            dve.wait_ge(lat_split, START + CHUNKS)
            nc.vector.tensor_reduce(c_maxb[:, :], c_max[:, :].rearrange("p (b c) -> p b c", b=B), AX.X, ALU.max
                                    ).then_inc(bound_w_ready, 1)
            dve.wait_ge(bound_w_ps, 1)
            for b in range(B):
                nc.vector.tensor_scalar(bound_w[:, b, :], head_of_row[:, :], ps[:, 7, b:b + 1], None, ALU.mult
                                        ).then_inc(bound_w_ready, 1)
            for b in range(B):
                dve.wait_ge(q_stored[b], Q_STORES * (1 + CHUNKS // 2))
                if b:
                    dve.wait_ge(shift_split, b)
                else:
                    dve.wait_ge(q_split, CHUNKS)
                dve.wait_ge(bound_ps, b + 1)
                split_shift(P, b, b, shift_split, shift_min[:, b:b + 1])
            dve.wait_ge(shift_split, B)
            nc.vector.tensor_reduce(shift_min[:, B:B + 1], shift_min[:, 0:B], AX.X, ALU.min).then_inc(min_ready, 1)
            dve.wait_ge(tight_ps, 1)
            ch = Chain(v_set)
            ch.then(nc.vector.tensor_reduce(tight_f[:, :], ps[0:1, 7, 0:P], AX.X, ALU.min))
            ch.end()
            nc.vector.tensor_scalar(tight[:, :], tight_f[:, :], -BOUND_LIMIT, None, ALU.is_ge).then_inc(tight_ok, 1)
            dve.wait_ge(tight_ok, 1)
            with dve.If(dve.value_load(tight[:, :], min_val=0, max_val=1) < 1):
                dve.wait_ge(shift_stored, SHIFTS)
                with dve.Fori(0, CHUNKS) as c:
                    with dve.Fori(0, G4) as g:
                        for u in range(4 * TT):
                            dve.wait_ge(m_scores, u + 1)
                            nc.vector.tensor_reduce(row_max[:, u % TT, bass.ds(g * 4 + u // TT, 1)],
                                                    ps[:, 4 * (u % 2):4 * (u % 2) + KT // 4, :], AX.XY, ALU.max
                                                    ).then_inc(m_max, 1)
                        dve.sem_inc(m_scores, -4 * TT)
                    dve.wait_ge(m_sum_ps, 1)
                    dve.sem_inc(m_sum_ps, -1)
                    split_shift(H, 6, 0, m_split)

            dve.wait_ge(prep_ps, 1)
            nc.vector.tensor_copy(wvbv_t, ps[:, prep_bank(1), 0:G4 * L + G4]).then_inc(prep_ok, 1)
            ch = Chain(v_set)
            ch.put(nc.vector.memset(lv[:, :, :], 0.0))
            ch.put(nc.vector.memset(bv_wide[:, :, :], 0.0))
            ch.wait()
            ch.end()
            dve.wait_ge(prep_ok, 1)
            for g in range(G4):
                for h in range(4):
                    at = 16 * (g % 2) + L * h
                    nc.vector.tensor_copy(lv[32 * h:32 * h + 32, g, at:at + L], wv_t[32 * h:32 * h + 32, g, :])
            nc.vector.tensor_copy(bv_wide[:, :, 0:1], bv_col.unsqueeze(2)).then_inc(prep_ok, 1)
            for half in range(2):
                m = PREP_LORA + half
                dve.wait_ge(prep_ps, m)
                nc.vector.tensor_scalar(lora_bt[:, bass.ts(half, N)], ps[:, prep_bank(m), :], coef, LORA_SCALE,
                                        ALU.mult, ALU.mult).then_inc(prep_ok, 1)
            for half in range(2):
                m = PREP_VO + half
                dve.wait_ge(prep_ps, m)
                split_three_pass(w_vo[:, 0, bass.ts(half, N)], w_vo[:, 1, bass.ts(half, N)], ps[:, prep_bank(m), :], prep_ok)
            for half in range(2):
                m = PREP_PART + half
                dve.wait_ge(prep_ps, m)
                nc.vector.tensor_copy(part_f[:, m % 2, :], ps[:, prep_bank(m), :]).then_inc(prep_ok, 1)
            for half in range(2):
                m = PREP_BIAS + half
                dve.wait_ge(prep_ps, m)
                nc.vector.tensor_tensor(attn_bias[:, bass.ts(half, N)], ps[:, prep_bank(m), :], attn_bias[:, bass.ts(half, N)],
                                        ALU.add).then_inc(prep_ok, 1)

            def move_w(k):
                m, kb, cols = PREP_W + k, k % KB, bass.ts(k // KB, N)
                dve.wait_ge(prep_ps, m)
                split_three_pass(w_eff[:, 0, kb, cols], w_eff[:, 1, kb, cols], ps[:, prep_bank(m), :], prep_ok)

            def move_o(c, half, first=False):
                dve.wait_ge(pv_done, (c * 2 + half + 1) * 4 * KT)
                if not first:
                    dve.wait_ge(o_turned, c * 2 + half)
                nc.vector.tensor_copy(o_sb[:, :], ps[:, 4 + half, :]).then_inc(o_moved, 1)

            def norm_o(c, half):
                dve.wait_ge(o_turned, c * 2 + half + 1)
                dve.wait_ge(o_back, START + c)
                turned = ps[:, 7, :].rearrange("p (t h m) -> p t h m", t=TT, h=4)[:, :, :, 0:4 * W5]
                turned = turned.rearrange("p t h (g d) -> p t h g d", d=W5)
                nc.vector.reciprocal(recip[:, :, :, :], turned[:, :, :, :, L]).then_inc(v_rec, 1)
                dve.wait_ge(v_rec, c * 2 + half + 1)
                for t in range(TT):
                    last = nc.vector.tensor_tensor(
                        o_q[:, t, 64 * half:64 * half + 64].rearrange("p (g h d) -> p h g d", h=4, d=L),
                        turned[:, t, :, :, 0:L], recip[:, t, :, :].unsqueeze(3).to_broadcast([P, 4, 4, L]), ALU.mult)
                last.then_inc(o_normed, 1)

            def split_o(p):
                dve.wait_ge(proj_ready, START + p * 2 * TT)
                dve.wait_ge(o_back, START + p + 1)
                split_three_pass(o_t[:, 0, :], o_t[:, 1, :], ps[:, 6, :], o_t_ready)

            def residual(p, t, at):
                dve.wait_ge(xb_ready, p * TT + t + 1)
                for n in range(2):
                    dve.wait_ge(proj_ready, START + (p * TT + t) * 2 + n + 1)
                    nc.vector.tensor_tensor(y[:, t, bass.ts(n, N)], ps[:, at + n, :], y[:, t, bass.ts(n, N)], ALU.add
                                            ).then_inc(y_ready, 1)

            def move_xn(p, t, banks):
                dve.wait_ge(ffn_ready, START + (p * TT + max(t - 1, 0)) * 2)
                for u in range(2):
                    dve.wait_ge(t_ready, START + CHUNKS * KB + (p * TT + t) * 2 + u + 1)
                    split_three_pass(xn_t[:, t % 2, 0, 4 * u:4 * u + 4, :].rearrange("p a n -> p (a n)"),
                                     xn_t[:, t % 2, 1, 4 * u:4 * u + 4, :].rearrange("p a n -> p (a n)"),
                                     ps[:, banks[u], :], t_moved)

            def add_dense(p, t):
                dve.wait_ge(yb_ready, p * TT + t + 1)
                for half in range(2):
                    dve.wait_ge(ffn_ready, START + (p * TT + t) * 2 + half + 1)
                    nc.vector.tensor_tensor(y[:, t, bass.ts(half, N)], ps[:, 6 + half, :], y[:, t, bass.ts(half, N)], ALU.add
                                            ).then_inc(ffn_moved, 1)

            for k in range(4):
                move_w(k)
            move_o(0, 0, True)
            norm_o(0, 0)
            for k in range(4, 2 * KB):
                move_w(k)
            with dve.Fori(1, CHUNKS) as c:
                p = c - 1
                move_o(p, 1)
                norm_o(p, 1)
                split_o(p)
                for t in range(TT):
                    residual(p, t, 6)
                dve.wait_ge(y_ready, START + c * 2 * TT)
                dve.wait_ge(t_ready, START + CHUNKS * KB + p * UNITS)
                layernorm(y, xn)
                for g in range(1, 2 + TT):
                    if g == 4:
                        move_o(c, 0)
                        norm_o(c, 0)
                    if g <= TT:
                        move_xn(p, g - 1, (7, 7))
                    if g >= 2:
                        add_dense(p, g - 2)
            p = CHUNKS - 1
            move_o(p, 1)
            norm_o(p, 1)
            split_o(p)
            dve.wait_ge(t_ready, START + CHUNKS * KB + p * UNITS)
            for t in range(TT):
                residual(p, t, 2 * (t % 2))
                dve.wait_ge(y_ready, START + (p * TT + t + 1) * 2)
                layernorm(y, xn, tiles=range(t, t + 1))
                if t == TT - 1:
                    add_dense(p, 0)
                if t:
                    move_xn(p, t - 1, (4, 5))
            add_dense(p, 1)
            move_xn(p, TT - 1, (4, 5))
            for t in range(2, TT):
                add_dense(p, t)


_INS = ["L0_attn_x", "L0_attn_Wq_d", "L0_attn_bq_d", "L0_attn_W_qk", "L0_attn_b_qk", "L0_attn_Wkv_d", "L0_attn_bkv_d",
        "L0_attn_Wv_u", "L0_attn_bv_u", "L0_attn_Wo", "L0_attn_bo", "L0_ffn_lora_A", "L0_ffn_lora_B", "L0_ffn_W",
        "L0_ffn_bias", "L0_ffn_lora_weights"]


def kernel(**inputs):
    import numpy as _np
    import concourse.bacc as _bacc
    from concourse import mybir as _mybir
    from concourse.bass_utils import run_bass_kernel_spmd as _run

    nc = _bacc.Bacc("TRN2", target_bir_lowering=False, num_devices=1)
    arrays, args = {}, []
    for name in _INS:
        a = _np.ascontiguousarray(inputs[name])
        arrays[f"in_{name}_dram"] = a
        args.append(nc.dram_tensor(f"in_{name}_dram", a.shape, _mybir.dt.from_np(a.dtype), kind="ExternalInput").ap())
    shape = inputs["L0_attn_x"].shape
    args.append(nc.dram_tensor("out_0_dram", shape, F32, kind="ExternalOutput").ap())
    build_block(nc, *args)
    r = _run(nc, [arrays], core_ids=[0])
    return r.results[0]["out_0_dram"]
```

```python
from contextlib import ExitStack

import concourse.bass as bass
from concourse import mybir

F32 = mybir.dt.float32
F32R = mybir.dt.float32r
BF16 = mybir.dt.bfloat16
I32 = mybir.dt.int32
ALU = mybir.AluOpType
ACT = mybir.ActivationFunctionType
AX = mybir.AxisListType

P = 128
N = 512


def build_block(nc, x, wq_d, bq_d, w_qk, b_qk, wkv_d, bkv_d, wv_u, bv_u, wo, bo,
                lora_a, lora_b, w_ffn, bias_ffn, lora_w, out):
    B, S, D = x.shape
    QL = wq_d.shape[1]
    L = wkv_d.shape[1]
    H = w_qk.shape[1] // L
    HD = wv_u.shape[1] // H
    NL, RANK = lora_a.shape[0], lora_a.shape[1]
    LORA_SCALE = 2.0
    EPS = 1e-5
    SCALE = L ** -0.5
    BOUND_LIMIT = 30.0
    T = B * S
    CHUNKS = T // N
    CB = S // N
    TT = N // P
    KT = S // P
    KB = D // P
    G4 = H // 4
    W5 = L + 1
    PARTS = 3
    ROWS = PARTS * W5
    QROW = 96
    assert H * L == P and NL * RANK == P and D == 2 * N and HD == 32

    x_t = x.rearrange("b s d -> (b s) d").rearrange("(t p) d -> t p d", p=P)
    out_t = out.rearrange("b s d -> (b s) d").rearrange("(t p) d -> t p d", p=P)
    qd = nc.dram_tensor("q_parts", [H, ROWS, T], BF16, kind="Internal").ap()

    with ExitStack() as ctx:
        def sb(name, shape, dt):
            return ctx.enter_context(nc.sbuf_tensor(name, shape, dt))

        def sem(name):
            return ctx.enter_context(nc.semaphore(name))

        ps = ctx.enter_context(nc.psum_tensor("ps", [P, 8, N], F32))

        ident = sb("ident", [P, P], F32)
        ones = sb("ones", [P, P], F32)
        head_of_row = sb("head_of_row", [P, H], F32)
        w_down = sb("w_down", [P, KB, 32], F32)
        fold = sb("fold", [P, 32], F32)
        spread = sb("spread", [P, P], F32)
        down_bias = sb("down_bias", [P, 1], F32)
        wqk_sb = sb("wqk_sb", [P, P], F32)
        bqk_sb = sb("bqk_sb", [P, 2], F32)
        sel_latent = sb("sel_latent", [P, P], F32)
        lora_a_sb = sb("lora_a_sb", [P, D], F32)
        lora_bt = sb("lora_bt", [P, D], F32)
        lv = sb("lv", [P, G4, 32], F32)
        bv_wide = sb("bv_wide", [P, G4, 32], F32)
        attn_bias = sb("attn_bias", [P, D], F32)
        ffn_bias = sb("ffn_bias", [P, D], F32)
        w_vo = sb("w_vo", [P, 2, D], F32R)
        o_t = sb("o_t", [P, 2, N], F32R)
        xn_t_at = nc.sbuf_base
        xn_t = sb("xn_t", [P, 2, 2, KB, P], F32R)
        q_abs = nc.alloc_sbuf_tensor_at("q_abs", [P, CHUNKS, N], F32, offset=xn_t_at)
        AREA = 2 * KB * D
        area_at = nc.sbuf_base
        area = sb("area", [P, AREA], F32)
        w_eff = nc.alloc_sbuf_tensor_at("w_eff", [P, 2, KB, D], F32R, offset=area_at)
        q_f32 = area[:, 0:T]
        xn_b = area[:, T:T + TT * D].rearrange("p (t d) -> p t d", t=TT)
        xt_b = area[:, T + TT * D:T + 2 * TT * D].rearrange("p (t d) -> p t d", t=TT)
        x_turned = area[:, T + 2 * TT * D:T + 2 * TT * D + KB * N].rearrange("p (k n) -> p k n", k=KB)
        key_t = sb("key_t", [P, T], BF16)
        CW = 3 * W5
        c_wide = sb("c_wide", [P, T // P, CW + 32], F32)
        q_in = sb("q_in", [P, 2, 4, N], BF16)
        probs_at = nc.sbuf_base
        probs = sb("probs", [P, 2, 4 * N], F32)
        lat = nc.alloc_sbuf_tensor_at("lat", [P, 2, N], F32, offset=probs_at)
        down_part = nc.alloc_sbuf_tensor_at("down_part", [P, N], F32, offset=probs_at + 4 * 2 * N)
        part_b = nc.alloc_sbuf_tensor_at("part_b", [P, 2, N], BF16, offset=probs_at + 4 * 3 * N)
        q_parts = nc.alloc_sbuf_tensor_at("q_parts_sb", [P, 2, PARTS, N], BF16, offset=probs_at + 4 * 4 * N)
        part_f = sb("part_f", [P, 2, N], F32)
        o_sb = sb("o_sb", [P, N], F32)
        o_q = sb("o_q", [P, TT, H * L], F32)
        recip = sb("recip", [P, TT, 4, 4], F32)
        y = sb("y", [P, TT, D], F32)
        xn = sb("xn", [P, TT, D], F32)
        stats = sb("stats", [P, TT, 2, 6], F32)
        mv = sb("mv", [P, TT, 2], F32)
        nw = sb("nw", [P, 2, 4, TT], F32)
        shift_f = sb("shift_f", [P, 2, N], F32)
        shift_parts = sb("shift_parts", [P, PARTS, N], BF16)
        c_max = sb("c_max", [P, CHUNKS], F32)
        c_maxb = sb("c_maxb", [P, B], F32)
        bound_w = sb("bound_w", [P, B, H], F32)
        small = sb("small", [P, 512], F32)
        shift_min = sb("shift_min", [P, B + 1], F32)
        tight_f = sb("tight_f", [1, 1], F32)
        tight = sb("tight", [1, 1], I32)
        row_max = sb("row_max", [P, TT, H], F32)

        x_tiles = [y, xt_b]
        xn_tiles = [xn, xn_b]
        w_stage = [y, xn]
        lora_b_sb = xn_b[:, 0, :].rearrange("p (a n r) -> p a n r", a=KB, n=NL)
        wv_in = xn_b[0:L, 1, :]
        wkv_in = small[:, 0:KB * L].rearrange("p (k n) -> p k n", k=KB)
        wq_in = small[:, 32:32 + KB * QL].rearrange("p (k n) -> p k n", k=KB)
        coef = small[:, 136:137]
        wvbv_t = small[:, 144:144 + G4 * L + G4]
        wv_t = wvbv_t[:, 0:G4 * L].rearrange("p (g n) -> p g n", g=G4)
        bv_col = wvbv_t[:, G4 * L:G4 * L + G4]
        bias_row = small[0:1, 192:192 + P]
        bkv_row = small[0:1, 320:320 + L]
        bq_row = small[0:1, 330:330 + QL]
        bv_rows = small[0:G4, 384:384 + P]

        w_in = sem("w_in")
        lora_in = sem("lora_in")
        stage_in = [sem("stage_in0"), sem("stage_in1")]
        const_ok = sem("const_ok")
        zero_ok = sem("zero_ok")
        pool_zero = sem("pool_zero")
        q_zero = sem("q_zero")
        bias_ps = sem("bias_ps")
        down_ok = sem("down_ok")
        v_set, v_ln, v_lat, v_shift, v_rec, v_hi = (sem(n) for n in ("v_set", "v_ln", "v_lat", "v_shift", "v_rec", "v_hi"))
        prep_ps = sem("prep_ps")
        prep_ok = sem("prep_ok")
        x_in = [[sem(f"x_in{half}_{t}") for t in range(TT)] for half in range(2)]
        norm_ready = sem("norm_ready")
        xn_ready = sem("xn_ready")
        t_ready = sem("t_ready")
        t_moved = sem("t_moved")
        down_done = sem("down_done")
        part_ready = sem("part_ready")
        spread_ps = sem("spread_ps")
        lat_ready = sem("lat_ready")
        q_ps = sem("q_ps")
        caug_ps = sem("caug_ps")
        caug_ready = sem("caug_ready")
        lat_split = sem("lat_split")
        q_read = sem("q_read")
        q_here = [sem("q_here0"), sem("q_here1")]
        p_own = sem("p_own")
        q_split = sem("q_split")
        q_stored = [sem("q_stored0"), sem("q_stored1")]
        abs_ready = sem("abs_ready")
        bound_w_ps = sem("bound_w_ps")
        bound_w_ready = sem("bound_w_ready")
        bound_ps = sem("bound_ps")
        shift_split = sem("shift_split")
        first_shift = sem("first_shift")
        shift_stored = sem("shift_stored")
        c_max_ready = sem("c_max_ready")
        min_ready = sem("min_ready")
        tight_ps = sem("tight_ps")
        tight_ok = sem("tight_ok")
        m_loaded = sem("m_loaded")
        m_scores = sem("m_scores")
        m_max = sem("m_max")
        m_abs = sem("m_abs")
        m_used = sem("m_used")
        m_sum_ps = sem("m_sum_ps")
        m_split = sem("m_split")
        m_read = sem("m_read")
        m_stored = sem("m_stored")
        m_reloaded = sem("m_reloaded")
        q_loaded = [sem("q_loaded0"), sem("q_loaded1")]
        s_ready = sem("s_ready")
        exp_done = sem("exp_done")
        pv_done = sem("pv_done")
        o_moved = sem("o_moved")
        o_turned = sem("o_turned")
        o_normed = sem("o_normed")
        o_back = sem("o_back")
        o_t_ready = sem("o_t_ready")
        proj_ready = sem("proj_ready")
        y_ready = sem("y_ready")
        ffn_ready = sem("ffn_ready")
        ffn_moved = sem("ffn_moved")
        x_back = [sem(f"x_back{t}") for t in range(TT)]
        xb_ready = sem("xb_ready")
        yb_ready = sem("yb_ready")
        out_done = [sem(f"out_done{t}") for t in range(TT)]

        block = ctx.enter_context(nc.Block())

        W_IN = 6 * 16
        LORA_IN = (6 + KB) * 16
        PAIRS = 2 * KT
        UNITS = 2 * TT
        START = 2
        START_AT_2 = (t_moved, lat_ready, caug_ready, q_read, lat_split, caug_ps, q_ps, part_ready, spread_ps,
                      t_ready, ffn_moved, y_ready, proj_ready, o_back, ffn_ready)
        Q_STORES = 16 * PARTS
        SHIFTS = 16 * PARTS * (CHUNKS - 1)
        SHIFTS_0 = 16 * PARTS * (CB - 1)
        SCORE_SLOTS = 3
        SUMS, SHARED = 6, 7
        TILE_STEPS = 2 + 3 * KB
        TURN_AT = 18 + 2 * TILE_STEPS
        TILE_AT = [18, 18 + TILE_STEPS, TURN_AT + 2, TURN_AT + 2 + TILE_STEPS]
        STORE_AT = [min(-(-(at + TILE_STEPS) // KT), G4 - 1) for at in TILE_AT]
        LOAD_AT = [min(g + 1, G4 - 1) for g in STORE_AT]
        PREP_LORA, PREP_VO, PREP_PART, PREP_BIAS, PREP_W = 2, 4, 6, 8, 10
        PREP_ALL = PREP_W + 4 * KB

        @block.sync
        def _(sp):
            for s in START_AT_2:
                sp.sem_inc(s, START)
            for slot in range(2):
                sp.sem_inc(q_stored[slot], Q_STORES)
            def first_tiles(half):
                for t in range(TT):
                    sp.dma_start(x_tiles[half][:, t, :], x_t[half * TT + t]).then_inc(x_in[half][t], 16)

            first_tiles(0)
            sp.dma_start(wkv_in, wkv_d.rearrange("(k p) n -> p k n", p=P)).then_inc(w_in, 16)
            sp.dma_start(wq_in, wq_d.rearrange("(k p) n -> p k n", p=P)).then_inc(w_in, 16)
            sp.dma_start(wqk_sb[QROW:QROW + QL, :], w_qk).then_inc(w_in, 16)
            sp.dma_start(bq_row, bq_d.rearrange("(a n) -> a n", a=1)).then_inc(w_in, 16)
            sp.dma_start(bkv_row, bkv_d.rearrange("(a n) -> a n", a=1)).then_inc(w_in, 16)
            sp.dma_start(bqk_sb[:, 0:1], b_qk.rearrange("(p a) -> p a", a=1)).then_inc(w_in, 16)
            first_tiles(1)
            sp.dma_start(bv_rows, bv_u.rearrange("(g p) -> g p", p=P)).then_inc(lora_in, 16)
            sp.dma_start(coef, lora_w.rearrange("(n a b) -> n a b", a=1, b=1).to_broadcast([NL, RANK, 1])
                         ).then_inc(lora_in, 16)
            sp.dma_start(attn_bias[:, :], bo.rearrange("(a n) -> a n", a=1).to_broadcast([P, D])).then_inc(lora_in, 16)
            sp.dma_start(ffn_bias[:, :], bias_ffn.rearrange("(a n) -> a n", a=1).to_broadcast([P, D])).then_inc(lora_in, 16)
            sp.dma_start(lora_a_sb[:, :], lora_a.rearrange("n r d -> (n r) d")).then_inc(lora_in, 16)

            def load_tiles(c, half):
                for t in range(TT):
                    sp.wait_ge(xn_ready, c * TT + t + 1)
                    sp.dma_start(x_tiles[half][:, t, :], x_t[(c + 2) * TT + t]).then_inc(x_in[half][t], 16)

            def store_q(c, slot):
                sp.wait_ge(q_split, c + 1)
                for k in range(PARTS):
                    sp.dma_start(qd[:, k * W5:k * W5 + L, bass.ds(c * N, N)], q_parts[:, slot, k, :]).then_inc(q_stored[slot], 16)

            for half in range(2):
                load_tiles(half, half)
            with sp.Fori(1, CHUNKS // 2 - 1) as i:
                for half in range(2):
                    load_tiles(i * 2 + half, half)
                    store_q(i * 2 + half - 2, half)
            def store_shifts(b):
                sp.wait_ge(shift_split, b + 1)
                for j in range(CB):
                    for k in range(PARTS):
                        sp.dma_start(qd[:, k * W5 + L, (b * CB + j) * N:(b * CB + j + 1) * N],
                                     shift_parts[32 * j:32 * j + H, k, :]
                                     ).then_inc(first_shift if b + j == 0 else shift_stored, 16)

            def load_q(c, g, slot, done):
                src = qd[bass.ds(g * 4, 4), :, bass.ds(c * N, N)].rearrange("h r n -> r h n")
                for j in range(PARTS):
                    sp.dma_start(q_in[32 * j:32 * j + ROWS, slot], src).then_inc(done, 16)

            for c in (CHUNKS - 4, CHUNKS - 3):
                store_q(c, c % 2)
            store_shifts(0)
            sp.wait_ge(q_stored[0], Q_STORES * (CHUNKS // 2))
            sp.wait_ge(first_shift, PARTS * 16)
            sp.wait_ge(q_zero, 1)
            load_q(0, 0, 0, q_loaded[0])
            for c in (CHUNKS - 2, CHUNKS - 1):
                store_q(c, c % 2)
            store_shifts(1)
            for slot in range(2):
                sp.wait_ge(q_stored[slot], Q_STORES * (1 + CHUNKS // 2))
            sp.wait_ge(shift_stored, SHIFTS)
            sp.wait_ge(tight_ok, 1)
            with sp.If(sp.value_load(tight[:, :], min_val=0, max_val=1) < 1):
                with sp.Fori(0, CHUNKS) as c:
                    with sp.Fori(0, G4) as g:
                        load_q(c, g, 1, m_loaded)
                        sp.wait_ge(m_read, 1)
                        sp.sem_inc(m_read, -1)
                    sp.wait_ge(m_split, c + 1)
                    for k in range(PARTS):
                        sp.dma_start(qd[:, k * W5 + L, bass.ds(c * N, N)], shift_parts[0:H, k, :]).then_inc(m_stored, 16)
                    sp.wait_ge(m_stored, PARTS * 16)
                    sp.sem_inc(m_stored, -PARTS * 16)
                sp.wait_ge(q_loaded[0], PARTS * 16)
                load_q(0, 0, 0, m_reloaded)

            sp.wait_ge(t_ready, START + CHUNKS * KB)
            sp.dma_start(wv_in, wv_u).then_inc(lora_in, 16)
            for a in range(KB):
                sp.dma_start(lora_b_sb[:, a], lora_b[:, a * P:(a + 1) * P, :].rearrange("n o r -> o n r")
                             ).then_inc(lora_in, 16)
            for half in range(2):
                sp.dma_start(w_stage[half][:, :, :].rearrange("p t (a n) -> p (t a) n", n=N),
                             wo[:, half * N:(half + 1) * N].rearrange("(a p) n -> p a n", p=P)).then_inc(stage_in[half], 16)

            def load_w():
                for half in range(2):
                    sp.wait_ge(prep_ps, PREP_PART + half)
                    sp.dma_start(w_stage[half][:, :, :], w_ffn[half * 4 * P:(half + 1) * 4 * P, :]
                                 .rearrange("(a p) n -> p a n", p=P)).then_inc(stage_in[half], 16)

            def load_x(c, t, first):
                if first:
                    sp.wait_ge(prep_ps, PREP_W + 2 * KB - 1)
                else:
                    sp.wait_ge(out_done[t], c * 16)
                sp.dma_start(y[:, t, :], x_t[c * TT + t]).then_inc(x_back[t], 16)

            def store_out(p, t):
                sp.wait_ge(ffn_moved, START + (p * TT + t + 1) * 2)
                sp.dma_start(out_t[p * TT + t], y[:, t, :]).then_inc(out_done[t], 16)

            def beside_attention(c, first, last):
                for g in range(G4):
                    if not (first and g == 0):
                        sp.wait_ge(s_ready, PAIRS * (c * G4 + g))
                    if g < G4 - 1:
                        load_q(c, g + 1, (g + 1) % 2, q_loaded[(g + 1) % 2])
                    elif not last:
                        load_q(c + 1, 0, 0, q_loaded[0])
                    if first and g == 2:
                        load_w()
                    if not first:
                        for t in range(TT):
                            if g == STORE_AT[t]:
                                store_out(c - 1, t)
                    for t in range(TT):
                        if g == LOAD_AT[t]:
                            load_x(c, t, first)

            beside_attention(0, True, False)
            with sp.Fori(1, CHUNKS - 1) as c:
                beside_attention(c, False, False)
            beside_attention(CHUNKS - 1, False, True)
            for t in range(TT):
                store_out(CHUNKS - 1, t)
            for t in range(TT):
                sp.wait_ge(out_done[t], CHUNKS * 16)

        @block.gpsimd
        def _(pool):
            pool.memset(ident[:, :], 0.0).then_inc(pool_zero, 1)
            pool.wait_ge(pool_zero, 1)
            pool.affine_select(out=ident[:, :], in_=ident[:, :], compare_op=ALU.not_equal, fill=1.0, base=0,
                               pattern=[[-1, P]], channel_multiplier=1).then_inc(const_ok, 1)
            pool.memset(ones[:, :], 1.0).then_inc(const_ok, 1)
            pool.memset(w_down[:, :, :], 0.0).then_inc(const_ok, 1)
            pool.memset(spread[:, :], 0.0).then_inc(const_ok, 1)
            pool.memset(key_t[:, :], 0.0).then_inc(zero_ok, 1)
            pool.memset(c_wide[:, :, :], 0.0).then_inc(zero_ok, 1)
            pool.memset(q_in[:, :, :, :], 0.0).then_inc(q_zero, 1)
            with pool.Fori(0, CHUNKS // 2) as i:
                for slot in range(2):
                    cols = bass.ds((i * 2 + slot) * N, N)
                    rest, parts = part_f[:, 1, :], q_parts[:, slot]
                    pool.wait_ge(q_here[slot], 2)
                    pool.tensor_tensor(rest, q_f32[:, cols], parts[:, 0, :], ALU.subtract).then_inc(p_own, 1)
                    pool.wait_ge(p_own, 1)
                    pool.tensor_copy(parts[:, 1, :], rest).then_inc(p_own, 1)
                    pool.wait_ge(p_own, 2)
                    pool.tensor_tensor(parts[:, 2, :], rest, parts[:, 1, :], ALU.subtract).then_inc(p_own, 1)
                    pool.wait_ge(p_own, 3)
                    pool.sem_inc(q_here[slot], -2)
                    pool.sem_inc(p_own, -3)
                    pool.sem_inc(q_split, 1)
            pool.wait_ge(prep_ok, PREP_W)
            with pool.Fori(0, CHUNKS) as c:
                for t in range(TT):
                    pool.wait_ge(x_back[t], (c + 1) * 16)
                    pool.tensor_tensor(y[:, t, :], y[:, t, :], attn_bias[:, :], ALU.add).then_inc(xb_ready, 1)
                for t in range(TT):
                    pool.wait_ge(xn_ready, (CHUNKS + c) * TT + t + 1)
                    pool.tensor_tensor(y[:, t, :], y[:, t, :], ffn_bias[:, :], ALU.add).then_inc(yb_ready, 1)

        @block.scalar
        def _(act):
            act.sem_inc(down_done, KB)

            def normalise(c, slot, t):
                if t == 0:
                    act.wait_ge(norm_ready, c + 1)
                nc.scalar.activation(xn_tiles[slot][:, t, :], x_tiles[slot][:, t, :], ACT.Identity,
                                     bias=nw[:, slot, 2, t:t + 1], scale=nw[:, slot, 3, t:t + 1]).then_inc(xn_ready, 1)

            def move_turned(c, kb):
                act.wait_ge(t_ready, START + c * KB + kb + 1)
                act.wait_ge(down_done, c * KB + kb + 1)
                nc.scalar.activation(x_turned[:, kb, :], ps[:, kb % 4, :], ACT.Copy).then_inc(t_moved, 1)

            def move_latents(c, slot):
                act.wait_ge(lat_split, START + c - 1)
                act.wait_ge(spread_ps, START + c + 1)
                nc.scalar.activation(lat[:, slot, :], ps[:, 5, :], ACT.Identity, bias=down_bias[:, 0:1]
                                     ).then_inc(lat_ready, 1)

            def move_products(c, slot, rounds):
                act.wait_ge(caug_ps, START + c + 1)
                nc.scalar.activation(c_wide[:, bass.ds(c * TT, TT), CW:CW + W5],
                                     ps[:, 6, :].rearrange("p (t m) -> p t m", t=TT)[:, :, 0:W5], ACT.Copy
                                     ).then_inc(caug_ready, 1)
                act.wait_ge(q_stored[slot], Q_STORES * (rounds + 1))
                act.wait_ge(q_ps, START + c + 1)
                nc.scalar.activation(q_parts[:, slot, 0, :], ps[:, 7, :], ACT.Identity, bias=bqk_sb[:, 1:2], scale=SCALE
                                     ).then_inc(q_here[slot], 1)
                nc.scalar.activation(q_f32[:, bass.ds(c * N, N)], ps[:, 7, :], ACT.Identity, bias=bqk_sb[:, 1:2], scale=SCALE
                                     ).then_inc(q_here[slot], 1)
                nc.scalar.activation(q_abs[:, bass.ds(c, 1), :].rearrange("p a n -> p (a n)"), ps[:, 7, :], ACT.Abs,
                                     bias=bqk_sb[:, 1:2], scale=SCALE).then_inc(q_read, 1)

            def move_parts(c):
                act.wait_ge(spread_ps, START + c)
                act.wait_ge(down_done, (c + 2) * KB)
                nc.scalar.activation(down_part[:, :], ps[:, 4, :], ACT.Copy).then_inc(part_ready, 1)

            def move_chunk(c, slot, rounds, first=False, last=False):
                for kb in range(KB):
                    move_turned(c, kb)
                    if kb == 1 and not first:
                        move_parts(c - 1)
                    if kb in (0, 2, 4, 5) and not last:
                        if kb == 0 and not first:
                            act.wait_ge(t_ready, START + c * KB)
                        normalise(c + 1, 1 - slot, (0, 2, 4, 5).index(kb))
                    if kb == 4 and not first:
                        move_latents(c - 1, 1 - slot)
                    if kb == KB - 1 and not first:
                        move_products(c - 1, 1 - slot, rounds)

            for t in range(TT):
                normalise(0, 0, t)
            act.wait_ge(down_ok, 3)
            act.wait_ge(zero_ok, 2)
            move_chunk(0, 0, 0, first=True)
            with act.Fori(0, CHUNKS // 2 - 1) as i:
                for half in range(2):
                    move_chunk(i * 2 + half + 1, 1 - half, i)
            move_chunk(CHUNKS - 1, 1, CHUNKS // 2 - 1, last=True)
            move_parts(CHUNKS - 1)
            move_latents(CHUNKS - 1, 1)
            move_products(CHUNKS - 1, 1, CHUNKS // 2 - 1)
            act.wait_ge(tight_ok, 1)
            with act.If(act.value_load(tight[:, :], min_val=0, max_val=1) < 1):
                with act.Fori(0, CHUNKS) as c:
                    nc.scalar.activation(lat[:, 0, :], q_f32[:, bass.ds(c * N, N)], ACT.Abs).then_inc(m_abs, 1)
                    act.wait_ge(m_used, 1)
                    act.sem_inc(m_used, -1)

            def exps(c, first):
                for g in range(G4):
                    for kt in range(KT):
                        for pair in range(2):
                            i = 2 * kt + pair
                            act.wait_ge(s_ready, (c * G4 + g) * PAIRS + i + 1)
                            if first and g == 0 and i == 2:
                                for slot in range(2):
                                    act.wait_ge(q_stored[slot], Q_STORES * (1 + CHUNKS // 2))
                            if pair == 0 and not (first and g == 0 and kt < 2):
                                act.wait_ge(pv_done, (c * G4 + g) * KT + kt - 1)
                            nc.scalar.activation(probs[:, kt % 2, bass.ts(pair, 2 * N)],
                                                 ps[:, 2 * (i % SCORE_SLOTS):2 * (i % SCORE_SLOTS) + 2, :]
                                                 .rearrange("p a n -> p (a n)"),
                                                 ACT.Exp).then_inc(exp_done, 1)

            exps(0, True)
            with act.Fori(1, CHUNKS) as c:
                exps(c, False)

        @block.tensor
        def _(pe):
            pe.wait_ge(w_in, W_IN)
            pe.wait_ge(const_ok, 4)
            pe.wait_ge(down_ok, 1)
            nc.tensor.matmul(ps[:, 7, 0:1], bias_row, ones[0:1, 0:1], start=True, stop=True).then_inc(bias_ps, 1)
            pe.wait_ge(down_ok, 3)

            def turn_x(c, slot, kb):
                if kb >= 4:
                    pe.wait_ge(t_moved, START + c * KB + kb - 3)
                for t in range(TT):
                    last = nc.tensor.transpose(ps[:, kb % 4, bass.ts(t, P)], xn_tiles[slot][:, t, bass.ts(kb, P)], ident[:, :])
                last.then_inc(t_ready, 1)

            def down(c, k):
                pe.wait_ge(t_moved, START + c * KB + k + 1)
                if k == 0:
                    pe.wait_ge(part_ready, START + c)
                i = k % 4
                nc.tensor.matmul(ps[32 * i:32 * i + 32, 4, :], w_down[:, k, :], x_turned[:, k, :], start=(k < 4), stop=(k >= 4)
                                 ).then_inc(down_done, 1)

            def sum_parts(c):
                pe.wait_ge(part_ready, START + c + 1)
                pe.wait_ge(lat_ready, START + c)
                nc.tensor.matmul(ps[:, 5, :], spread[:, :], down_part[:, :], start=True, stop=True).then_inc(spread_ps, 1)

            def use_latents(c, slot):
                pe.wait_ge(lat_ready, START + c + 1)
                pe.wait_ge(caug_ready, START + c)
                for t in range(TT):
                    last = nc.tensor.transpose(ps[:, 6, bass.ts(t, P)], lat[:, slot, bass.ts(t, P)], ident[:, :])
                last.then_inc(caug_ps, 1)
                pe.wait_ge(q_read, START + c)
                nc.tensor.matmul(ps[:, 7, :], wqk_sb[QROW:QROW + QL, :], lat[QROW:QROW + QL, slot, :], start=True, stop=True
                                 ).then_inc(q_ps, 1)

            def largest(b):
                pe.wait_ge(c_max_ready, b + 1)
                nc.tensor.matmul(ps[:, 5, 0:1], sel_latent[:, :], c_maxb[:, b:b + 1], start=True, stop=True
                                 ).then_inc(bound_w_ps, 1)

            def bounds(b):
                pe.wait_ge(bound_w_ready, b + 1)
                for j in range(CB):
                    last = nc.tensor.matmul(ps[32 * j:32 * j + H, b, :], bound_w[:, b, :], q_abs[:, b * CB + j, :],
                                            start=True, stop=True)
                last.then_inc(bound_ps, 1)

            def stage1(c, slot, first=False, beside=None):
                pe.wait_ge(xn_ready, (c + 1) * TT)
                for kb in range(KB):
                    turn_x(c, slot, kb)
                    if kb < 2 and not first:
                        down(c - 1, KB - 2 + kb)
                    if kb >= 2:
                        down(c, kb - 2)
                    if kb == 3 and not first:
                        if beside is bounds:
                            pe.wait_ge(bound_w_ready, 1)
                        sum_parts(c - 1)
                    if kb == 6 and not first:
                        use_latents(c - 1, 1 - slot)
                if beside:
                    beside(0)

            stage1(0, 0, True)
            with pe.Fori(0, CHUNKS // 2 - 2) as i:
                for half in range(2):
                    stage1(i * 2 + half + 1, 1 - half)
            for c, beside in ((CHUNKS - 3, None), (CHUNKS - 2, largest), (CHUNKS - 1, bounds)):
                stage1(c, c % 2, beside=beside)
            for k in range(KB - 2, KB):
                down(CHUNKS - 1, k)
            sum_parts(CHUNKS - 1)
            use_latents(CHUNKS - 1, 1)
            largest(1)
            pe.wait_ge(q_read, START + CHUNKS)
            bounds(1)
            pe.wait_ge(min_ready, 1)
            nc.tensor.matmul(ps[0:1, 7, 0:P], shift_min[:, B:B + 1], ident[:, :], start=True, stop=True).then_inc(tight_ps, 1)
            pe.wait_ge(tight_ok, 1)
            with pe.If(pe.value_load(tight[:, :], min_val=0, max_val=1) < 1):
                for b in range(B):
                    with pe.Fori(b * CB, (b + 1) * CB) as c:
                        with pe.Fori(0, G4):
                            pe.wait_ge(m_loaded, PARTS * 16)
                            pe.sem_inc(m_loaded, -PARTS * 16)
                            for u in range(4 * TT):
                                if u >= 2:
                                    pe.wait_ge(m_max, u - 1)
                                for n in range(KT // 4):
                                    last = nc.tensor.matmul(ps[:, 4 * (u % 2) + n, :],
                                                            q_in[:, 1, u // TT, bass.ts(u % TT, P)],
                                                            key_t[:, b * S + n * N:b * S + (n + 1) * N], start=True, stop=True)
                                last.then_inc(m_scores, 1)
                            pe.wait_ge(m_max, 4 * TT)
                            pe.sem_inc(m_max, -4 * TT)
                            pe.drain().then_inc(m_read, 1)
                        pe.wait_ge(m_abs, 1)
                        pe.sem_inc(m_abs, -1)
                        nc.tensor.matmul(ps[0:H, 6, :], bound_w[:, b, :], lat[:, 0, :], start=True, stop=False).then_inc(m_used, 1)
                        for t in range(TT):
                            last = nc.tensor.matmul(ps[0:H, 6, bass.ts(t, P)], row_max[:, t, :], ident[:, :],
                                                    start=False, stop=(t == TT - 1))
                        last.then_inc(m_sum_ps, 1)
                        pe.wait_ge(m_split, c + 1)
                pe.wait_ge(m_reloaded, PARTS * 16)
            def free_bank(m):
                pe.wait_ge(prep_ok, m)

            def turn_values():
                pe.wait_ge(lora_in, LORA_IN)
                for g in range(G4):
                    nc.tensor.transpose(ps[:, SHARED, bass.ts(g, L)], wv_in[:, bass.ts(g, P)], ident[0:L, 0:L])
                nc.tensor.transpose(ps[:, SHARED, G4 * L:G4 * L + G4], bv_rows, ident[0:G4, 0:G4]).then_inc(prep_ps, 1)

            def turn_lora(m):
                free_bank(m)
                for a in range(4):
                    last = nc.tensor.transpose(ps[:, SHARED, bass.ts(a, P)],
                                               lora_b_sb[:, (m - PREP_LORA) * 4 + a].rearrange("p n r -> p (n r)"), ident[:, :])
                last.then_inc(prep_ps, 1)

            def times_wo(m, weights, odd):
                half = m % 2
                if odd == 0:
                    free_bank(m)
                    pe.wait_ge(stage_in[half], 16)
                for g in range(odd, G4, 2):
                    i = g // 2
                    last = nc.tensor.matmul(ps[32 * i:32 * i + 32, SHARED, :], weights[:, g, :],
                                            w_stage[half][:, g // 2, bass.ts(g % 2, N)], start=(odd == 0), stop=(odd == 1))
                if odd == 1:
                    last.then_inc(prep_ps, 1)

            def sum_bias(m):
                free_bank(m)
                nc.tensor.matmul(ps[:, SHARED, :], ones[:, :], part_f[:, m % 2, :], start=True, stop=True
                                 ).then_inc(prep_ps, 1)

            def turn_w(k):
                kb, half = k % KB, k // KB
                free_bank(PREP_W + 2 * k)
                pe.wait_ge(stage_in[half], 32)
                if k == 4:
                    pe.wait_ge(o_normed, 1)
                for a in range(4):
                    last = nc.tensor.transpose(ps[:, SHARED, bass.ts(a, P)], w_stage[half][:, a, bass.ts(kb, P)], ident[:, :])
                last.then_inc(prep_ps, 1)

            def lora_update(k):
                free_bank(PREP_W + 2 * k + 1)
                nc.tensor.matmul(ps[:, SHARED, :], lora_a_sb[:, bass.ts(k % KB, P)],
                                 lora_bt[:, bass.ts(k // KB, N)], start=True, stop=True).then_inc(prep_ps, 1)

            def prepare(g, kt):
                if g == 0 and kt == 7:
                    turn_values()
                if g == 0 and kt in (9, 12):
                    turn_lora(PREP_LORA + kt // 12)
                if g == 1 and kt % 2 == 0:
                    times_wo(PREP_VO + kt // 4, lv if kt < 8 else bv_wide, kt // 2 % 2)
                if g == 2 and kt in (4, 8):
                    sum_bias(PREP_BIAS + kt // 8)
                k, step = divmod((g - 3) * KT + kt, 5)
                if g >= 3 and step == 0:
                    turn_w(k)
                if g >= 3 and step == 2:
                    lora_update(k)

            def scores(c, b, g, kt, pair, first):
                i, at = 2 * kt + pair, 2 * ((2 * kt + pair) % SCORE_SLOTS)
                if i >= SCORE_SLOTS:
                    pe.wait_ge(exp_done, (c * G4 + g) * PAIRS + i - SCORE_SLOTS + 1)
                elif i < 2 and not (first and g == 0):
                    pe.wait_ge(exp_done, (c * G4 + g) * PAIRS - 1 + i)
                for h in (0, 1):
                    last = nc.tensor.matmul(ps[:, at + h, :], key_t[:, bass.ts(b * KT + kt, P)], q_in[:, g % 2, 2 * pair + h, :],
                                            start=True, stop=True)
                last.then_inc(s_ready, 1)

            def values(c, b, g, kt):
                at = CW - W5 * (g % 4)
                pe.wait_ge(exp_done, (c * G4 + g) * PAIRS + 2 * kt + 2)
                for h in range(4):
                    last = nc.tensor.matmul(ps[32 * h:32 * h + 32, SUMS, :], c_wide[:, b * KT + kt, at:at + 32],
                                            probs[:, kt % 2, bass.ts(h, N)], start=(kt == 0 and g % 4 == 0),
                                            stop=(kt == KT - 1 and g % 4 == 3))
                last.then_inc(pv_done, 1)

            def turn_o(c, half):
                pe.wait_ge(o_moved, 2 * c + half + 1)
                for t in range(TT):
                    last = nc.tensor.transpose(ps[:, SHARED, bass.ts(t, P)], o_sb[:, bass.ts(t, P)], ident[:, :])
                last.then_inc(o_turned, 1)

            THREE = ((0, 0), (0, 1), (1, 0))

            def turn_back(p):
                pe.wait_ge(o_normed, (p + 1) * 2)
                for t in range(TT):
                    last = nc.tensor.transpose(ps[:, SHARED, bass.ts(t, P)], o_q[:, t, :], ident[:, :])
                last.then_inc(o_back, 1)

            def project(p, t, n, bank):
                for i, (a, b) in enumerate(THREE):
                    last = nc.tensor.matmul(ps[:, bank, :], o_t[:, a, bass.ts(t, P)], w_vo[:, b, bass.ts(n, N)],
                                            start=(i == 0), stop=(i == 2))
                last.then_inc(proj_ready, 1)

            def turn_xn(p, t, u, bank):
                pe.wait_ge(xn_ready, (CHUNKS + p) * TT + t + 1)
                for a in range(4):
                    last = nc.tensor.transpose(ps[:, bank, bass.ts(a, P)], xn[:, t, bass.ts(4 * u + a, P)], ident[:, :])
                last.then_inc(t_ready, 1)

            def dense(p, t, half, kb, bank):
                for i, (a, b) in enumerate(THREE):
                    last = nc.tensor.matmul(ps[:, bank, :], xn_t[:, t % 2, a, kb, :], w_eff[:, b, kb, bass.ts(half, N)],
                                            start=(kb + i == 0), stop=(kb == KB - 1 and i == 2))
                if kb == KB - 1:
                    last.then_inc(ffn_ready, 1)

            def dense_beside(c, g, kt):
                p = c - 1
                if g == 0 and kt == 4:
                    turn_back(p)
                if g == 0 and 6 <= kt < 6 + 2 * TT:
                    t, n = divmod(kt - 6, 2)
                    if kt == 6:
                        pe.wait_ge(o_t_ready, p + 1)
                    else:
                        pe.wait_ge(y_ready, START + (p * TT + t) * 2 + n)
                    project(p, t, n, SHARED)
                for t in range(TT):
                    step = g * KT + kt - TILE_AT[t]
                    if step == 0:
                        if t == 2:
                            pe.wait_ge(o_normed, 2 * c + 1)
                        elif t:
                            pe.wait_ge(ffn_moved, START + (p * TT + t) * 2)
                        turn_xn(p, t, 0, SHARED)
                    elif step == 1:
                        pe.wait_ge(t_moved, START + CHUNKS * KB + (p * TT + t) * 2 + 1)
                        turn_xn(p, t, 1, SHARED)
                    elif 3 <= step < TILE_STEPS and step % 3 < 2:
                        half, kb = divmod((step - 3) // 3 * 2 + step % 3, KB)
                        if kb == 0 and half == 0:
                            pe.wait_ge(t_moved, START + CHUNKS * KB + (p * TT + t + 1) * 2)
                        elif kb == 0:
                            pe.wait_ge(ffn_moved, START + (p * TT + t) * 2 + 1)
                        dense(p, t, half, kb, SHARED)

            def attention(c, b, b_before=None):
                first = b_before is None
                for g in range(G4):
                    pe.wait_ge(q_loaded[g % 2], (c * (G4 // 2) + g // 2 + 1) * 16 * PARTS)
                    for kt in range(KT):
                        for pair in range(2):
                            scores(c, b, g, kt, pair, first)
                        if kt == 0 and g:
                            values(c, b, g - 1, KT - 1)
                        elif kt == 0 and not first:
                            values(c - 1, b_before, G4 - 1, KT - 1)
                        elif kt:
                            if kt == 1 and g % 4 == 0 and not (first and g == 0):
                                pe.wait_ge(o_moved, 2 * c + g // 4)
                            values(c, b, g, kt - 1)
                        if kt == 2 and g == 0 and not first:
                            pe.wait_ge(ffn_moved, START + (c - 1) * TT * 2)
                            turn_o(c - 1, 1)
                        if first and kt == 3 and g == 4:
                            pe.wait_ge(prep_ok, PREP_W + 8)
                            turn_o(c, 0)
                        if not first and g * KT + kt == TURN_AT:
                            pe.wait_ge(ffn_moved, START + ((c - 1) * TT + 2) * 2)
                            turn_o(c, 0)
                        if first:
                            prepare(g, kt)
                        else:
                            dense_beside(c, g, kt)

            attention(0, 0)
            pe.wait_ge(prep_ok, PREP_ALL)
            with pe.Fori(1, CB) as c:
                attention(c, 0, 0)
            attention(CB, 1, 0)
            with pe.Fori(CB + 1, CHUNKS) as c:
                attention(c, 1, 1)
            values(CHUNKS - 1, B - 1, G4 - 1, KT - 1)
            p = CHUNKS - 1
            turn_o(p, 1)
            turn_back(p)
            pe.wait_ge(exp_done, CHUNKS * G4 * PAIRS)
            pe.wait_ge(o_t_ready, p + 1)

            def project_last(t):
                if t >= 2:
                    pe.wait_ge(y_ready, START + (p * TT + t - 1) * 2)
                for n in range(2):
                    project(p, t, n, 2 * (t % 2) + n)

            def turn_last(t):
                for u in range(2):
                    if t:
                        pe.wait_ge(t_moved, START + CHUNKS * KB + (p * TT + t - 1) * 2 + u + 1)
                    turn_xn(p, t, u, 4 + u)

            project_last(0)
            project_last(1)
            turn_last(0)
            project_last(2)
            for t in range(TT):
                for half in range(2):
                    pe.wait_ge(t_moved, START + CHUNKS * KB + (p * TT + t + 1) * 2)
                    if t:
                        pe.wait_ge(ffn_moved, START + (p * TT + t) * 2 - 1 + half)
                    for kb in range(KB):
                        if half == 1 and kb == KB // 2 and t < TT - 1:
                            turn_last(t + 1)
                        dense(p, t, half, kb, 6 + half)
                if t == 0:
                    project_last(3)

        @block.vector
        def _(dve):
            class Chain:
                def __init__(self, s):
                    self.sem, self.n = s, 0

                def put(self, ins):
                    self.n += 1
                    ins.then_inc(self.sem, 1)

                def wait(self):
                    dve.wait_ge(self.sem, self.n)

                def then(self, ins):
                    self.put(ins)
                    self.wait()

                def end(self):
                    self.wait()
                    dve.sem_inc(self.sem, -self.n)

            def measure(ch, tile, t):
                for n in range(2):
                    ch.put(nc.vector.bn_stats(stats[:, t, n, :], tile[:, t, bass.ts(n, N)]))

            def deviations(ch, slot=0, tiles=range(TT)):
                ch.wait()
                for t in tiles:
                    ch.put(nc.vector.bn_aggr(mv[:, t, :], stats[:, t, :, :].rearrange("p n s -> p (n s)")))
                ch.wait()
                lo, hi = tiles[0], tiles[-1] + 1
                v, r, a = nw[:, slot, 0, lo:hi], nw[:, slot, 3, lo:hi], nw[:, slot, 1, lo:hi]
                ch.then(nc.vector.tensor_scalar(v, mv[:, lo:hi, 1], EPS, None, ALU.add))
                ch.then(nc.vector.tensor_scalar(a.bitcast(I32), v.bitcast(I32), 1, None, ALU.logical_shift_right))
                ch.then(nc.vector.tensor_scalar(r.bitcast(I32), a.bitcast(I32), -1.0, float(0x5F3759DF), ALU.mult, ALU.add))
                for _ in range(3):
                    ch.then(nc.vector.scalar_tensor_tensor(out=a, in0=r, scalar=-0.5, in1=r, op0=ALU.mult, op1=ALU.mult))
                    ch.then(nc.vector.tensor_tensor(a, a, v, ALU.mult))
                    ch.then(nc.vector.scalar_tensor_tensor(out=r, in0=a, scalar=1.5, in1=r, op0=ALU.add, op1=ALU.mult))
                ch.end()

            def normalise(tiles=range(TT)):
                for t in tiles:
                    nc.vector.tensor_scalar(xn[:, t, :], y[:, t, :], mv[:, t, 0:1], nw[:, 0, 3, t:t + 1],
                                            ALU.subtract, ALU.mult).then_inc(xn_ready, 1)

            def split_shift(rows, bank, done, smallest=None, then=None):
                ch = Chain(v_shift)
                shift, shift_r = shift_f[0:rows, 0, :], shift_f[0:rows, 1, :]
                parts = shift_parts[0:rows]
                ch.then(nc.vector.tensor_scalar(shift, ps[0:rows, bank, :], -1.0, None, ALU.mult))
                if smallest is not None:
                    ch.then(nc.vector.tensor_reduce(smallest, shift, AX.X, ALU.min))
                if then:
                    then()
                ch.then(nc.vector.tensor_copy(parts[:, 0, :], shift))
                ch.then(nc.vector.tensor_tensor(shift_r, shift, parts[:, 0, :], ALU.subtract))
                ch.then(nc.vector.tensor_copy(parts[:, 1, :], shift_r))
                ch.end()
                nc.vector.tensor_tensor(parts[:, 2, :], shift_r, parts[:, 1, :], ALU.subtract).then_inc(done, 1)

            def split_three_pass(high, low, bank_part, moved):
                ch = Chain(v_hi)
                ch.then(nc.vector.tensor_copy(high, bank_part))
                ch.end()
                nc.vector.tensor_tensor(low, bank_part, high.bitcast(F32), ALU.subtract).then_inc(moved, 1)

            def statistics(rounds, half):
                ch = Chain(v_ln)
                for t in range(TT):
                    dve.wait_ge(x_in[half][t], rounds * 16)
                    measure(ch, x_tiles[half], t)
                deviations(ch, half)
                nc.vector.scalar_tensor_tensor(out=nw[:, half, 2, :], in0=mv[:, :, 0], scalar=-1.0, in1=nw[:, half, 3, :],
                                               op0=ALU.mult, op1=ALU.mult).then_inc(norm_ready, 1)

            def split_latents(c, slot, meanwhile=None):
                ch = Chain(v_lat)
                cols = bass.ds(c * N, N)
                src = lat[:, slot, :]
                dve.wait_ge(lat_ready, START + c + 1)
                ch.put(nc.vector.tensor_copy(part_b[0:96, 0, :], src[0:96, :]))
                ch.put(nc.vector.tensor_reduce(c_max[:, bass.ds(c, 1)], src, AX.X, ALU.max, apply_absolute_value=True))
                ch.put(nc.vector.tensor_copy(key_t[0:32, cols], src[0:32, :]))
                ch.wait()
                if meanwhile:
                    meanwhile()
                ch.then(nc.vector.tensor_tensor(part_f[0:96, 0, :], src[0:96, :], part_b[0:96, 0, :], ALU.subtract))
                ch.put(nc.vector.tensor_copy(key_t[32:64, cols], part_f[32:64, 0, :]))
                ch.then(nc.vector.tensor_copy(part_b[64:96, 1, :], part_f[64:96, 0, :]))
                ch.end()
                nc.vector.tensor_tensor(key_t[64:96, cols], part_f[64:96, 0, :], part_b[64:96, 1, :], ALU.subtract
                                        ).then_inc(lat_split, 1)

            def largest(b):
                nc.vector.tensor_reduce(c_maxb[:, b:b + 1], c_max[:, bass.ts(b, CB)], AX.X, ALU.max).then_inc(c_max_ready, 1)

            def weigh(b):
                dve.wait_ge(bound_w_ps, b + 1)
                nc.vector.tensor_scalar(bound_w[:, b, :], head_of_row[:, :], ps[:, 5, 0:1], None, ALU.mult
                                        ).then_inc(bound_w_ready, 1)

            def judge():
                nc.vector.tensor_reduce(shift_min[:, B:B + 1], shift_min[:, 0:B], AX.X, ALU.min).then_inc(min_ready, 1)
                dve.wait_ge(tight_ps, 1)
                ch = Chain(v_set)
                ch.then(nc.vector.tensor_reduce(tight_f[:, :], ps[0:1, 7, 0:P], AX.X, ALU.min))
                ch.end()
                nc.vector.tensor_scalar(tight[:, :], tight_f[:, :], -BOUND_LIMIT, None, ALU.is_ge).then_inc(tight_ok, 1)
                dve.wait_ge(first_shift, PARTS * 16)
                dve.wait_ge(shift_stored, SHIFTS_0)

            dve.wait_ge(const_ok, 4)
            ch = Chain(v_set)
            ch.put(nc.vector.memset(bias_row, 0.0))
            ch.put(nc.vector.tensor_copy(sel_latent[:, :].rearrange("p (h d) -> p h d", d=L),
                                         ident[:, 0:L].unsqueeze(1).to_broadcast([P, H, L])))
            ch.put(nc.vector.tensor_reduce(head_of_row[:, :], ident[:, :].rearrange("p (h d) -> p h d", d=L), AX.X, ALU.add))
            ch.put(nc.vector.tensor_reduce(fold[:, :], ident[:, :].rearrange("p (i m) -> p m i", m=32), AX.X, ALU.add))
            ch.wait()
            for j in range(PARTS):
                ch.put(nc.vector.tensor_copy(spread[:, 32 * j:32 * j + 16], fold[:, 0:16]))
            ch.put(nc.vector.tensor_copy(spread[:, QROW:QROW + QL], fold[:, 16:16 + QL]))
            statistics(1, 0)
            dve.wait_ge(w_in, W_IN)
            ch.put(nc.vector.tensor_scalar(bqk_sb[:, 1:2], bqk_sb[:, 0:1], SCALE, None, ALU.mult))
            for i in range(PARTS):
                ch.put(nc.vector.tensor_copy(w_down[:, :, W5 * i:W5 * i + L], wkv_in))
                for j in range(PARTS):
                    col = 32 * j + W5 * i
                    ch.put(nc.vector.tensor_copy(bias_row[:, col:col + L], bkv_row))
                ch.put(nc.vector.memset(bias_row[:, W5 * i + L:W5 * i + W5], 1.0))
            ch.put(nc.vector.tensor_copy(w_down[:, :, 16:16 + QL], wq_in))
            ch.put(nc.vector.tensor_copy(bias_row[:, QROW:QROW + QL], bq_row))
            ch.wait()
            ch.end()
            dve.sem_inc(down_ok, 1)
            dve.wait_ge(bias_ps, 1)
            nc.vector.tensor_copy(down_bias[:, :], ps[:, 7, 0:1]).then_inc(down_ok, 1)
            dve.sem_inc(down_ok, 1)

            statistics(1, 1)
            dve.wait_ge(zero_ok, 2)
            dve.wait_ge(xn_ready, TT)
            statistics(2, 0)
            with dve.Fori(0, CHUNKS // 2 - 2) as i:
                for half in range(2):
                    dve.wait_ge(xn_ready, (i * 2 + half + 2) * TT)
                    statistics(i + 2 + half, 1 - half)
                    split_latents(i * 2 + half, half)
            dve.wait_ge(lat_split, START + CB)
            largest(0)
            dve.wait_ge(xn_ready, (CHUNKS - 2) * TT)
            statistics(CHUNKS // 2, 1)
            split_latents(CB, 0)
            weigh(0)
            split_latents(CB + 1, 1)
            split_latents(CB + 2, 0)
            dve.wait_ge(bound_ps, 1)
            split_shift(P, 0, shift_split, shift_min[:, 0:1])
            split_latents(CB + 3, 1, lambda: largest(1))
            weigh(1)
            dve.wait_ge(shift_split, 1)
            dve.wait_ge(bound_ps, 2)
            split_shift(P, 1, shift_split, shift_min[:, 1:2], judge)
            dve.wait_ge(tight_ok, 1)
            with dve.If(dve.value_load(tight[:, :], min_val=0, max_val=1) < 1):
                dve.wait_ge(shift_stored, SHIFTS)
                with dve.Fori(0, CHUNKS) as c:
                    with dve.Fori(0, G4) as g:
                        for u in range(4 * TT):
                            dve.wait_ge(m_scores, u + 1)
                            nc.vector.tensor_reduce(row_max[:, u % TT, bass.ds(g * 4 + u // TT, 1)],
                                                    ps[:, 4 * (u % 2):4 * (u % 2) + KT // 4, :], AX.XY, ALU.max
                                                    ).then_inc(m_max, 1)
                        dve.sem_inc(m_scores, -4 * TT)
                    dve.wait_ge(m_sum_ps, 1)
                    dve.sem_inc(m_sum_ps, -1)
                    split_shift(H, 6, m_split)

            dve.wait_ge(prep_ps, 1)
            nc.vector.tensor_copy(wvbv_t, ps[:, SHARED, 0:G4 * L + G4]).then_inc(prep_ok, 1)
            ch = Chain(v_set)
            ch.put(nc.vector.memset(lv[:, :, :], 0.0))
            ch.put(nc.vector.memset(bv_wide[:, :, :], 0.0))
            ch.wait()
            ch.end()
            dve.wait_ge(prep_ok, 1)
            for g in range(G4):
                for h in range(4):
                    at = 16 * (g % 2) + L * h
                    nc.vector.tensor_copy(lv[32 * h:32 * h + 32, g, at:at + L], wv_t[32 * h:32 * h + 32, g, :])
            nc.vector.tensor_copy(bv_wide[:, :, 0:1], bv_col.unsqueeze(2)).then_inc(prep_ok, 1)
            for half in range(2):
                m = PREP_LORA + half
                dve.wait_ge(prep_ps, m)
                nc.vector.tensor_scalar(lora_bt[:, bass.ts(half, N)], ps[:, SHARED, :], coef, LORA_SCALE,
                                        ALU.mult, ALU.mult).then_inc(prep_ok, 1)
            for half in range(2):
                m = PREP_VO + half
                dve.wait_ge(prep_ps, m)
                split_three_pass(w_vo[:, 0, bass.ts(half, N)], w_vo[:, 1, bass.ts(half, N)], ps[:, SHARED, :], prep_ok)
            for half in range(2):
                m = PREP_PART + half
                dve.wait_ge(prep_ps, m)
                nc.vector.tensor_copy(part_f[:, m % 2, :], ps[:, SHARED, :]).then_inc(prep_ok, 1)
            for half in range(2):
                m = PREP_BIAS + half
                dve.wait_ge(prep_ps, m)
                nc.vector.tensor_tensor(attn_bias[:, bass.ts(half, N)], ps[:, SHARED, :], attn_bias[:, bass.ts(half, N)],
                                        ALU.add).then_inc(prep_ok, 1)

            def move_w(k):
                m, kb, cols = PREP_W + 2 * k, k % KB, bass.ts(k // KB, N)
                base = part_f[:, k % 2, :]
                dve.wait_ge(prep_ps, m)
                nc.vector.tensor_copy(base, ps[:, SHARED, :]).then_inc(prep_ok, 1)
                dve.wait_ge(prep_ok, m + 1)
                dve.wait_ge(prep_ps, m + 1)
                ch = Chain(v_set)
                ch.then(nc.vector.tensor_tensor(base, ps[:, SHARED, :], base, ALU.add))
                ch.end()
                split_three_pass(w_eff[:, 0, kb, cols], w_eff[:, 1, kb, cols], base, prep_ok)

            def move_o(c, half, first=False):
                dve.wait_ge(pv_done, (c * 2 + half + 1) * 4 * KT)
                if not first:
                    dve.wait_ge(o_turned, c * 2 + half)
                nc.vector.tensor_copy(o_sb[:, :], ps[:, SUMS, :]).then_inc(o_moved, 1)

            def norm_o(c, half):
                dve.wait_ge(o_turned, c * 2 + half + 1)
                dve.wait_ge(o_back, START + c)
                turned = ps[:, SHARED, :].rearrange("p (t h m) -> p t h m", t=TT, h=4)[:, :, :, 0:4 * W5]
                turned = turned.rearrange("p t h (g d) -> p t h g d", d=W5)
                nc.vector.reciprocal(recip[:, :, :, :], turned[:, :, :, :, L]).then_inc(v_rec, 1)
                dve.wait_ge(v_rec, c * 2 + half + 1)
                for t in range(TT):
                    last = nc.vector.tensor_tensor(
                        o_q[:, t, 64 * half:64 * half + 64].rearrange("p (g h d) -> p h g d", h=4, d=L),
                        turned[:, t, :, :, 0:L], recip[:, t, :, :].unsqueeze(3).to_broadcast([P, 4, 4, L]), ALU.mult)
                last.then_inc(o_normed, 1)

            def split_o(p):
                dve.wait_ge(proj_ready, START + p * 2 * TT)
                dve.wait_ge(o_back, START + p + 1)
                split_three_pass(o_t[:, 0, :], o_t[:, 1, :], ps[:, SHARED, :], o_t_ready)

            def residual(p, t, banks, ch):
                dve.wait_ge(xb_ready, p * TT + t + 1)
                for n in range(2):
                    dve.wait_ge(proj_ready, START + (p * TT + t) * 2 + n + 1)
                    nc.vector.tensor_tensor(y[:, t, bass.ts(n, N)], ps[:, banks[n], :], y[:, t, bass.ts(n, N)], ALU.add
                                            ).then_inc(y_ready, 1)
                dve.wait_ge(y_ready, START + (p * TT + t + 1) * 2)
                measure(ch, y, t)

            def move_xn(p, t, banks):
                dve.wait_ge(ffn_ready, START + (p * TT + max(t - 1, 0)) * 2)
                for u in range(2):
                    dve.wait_ge(t_ready, START + CHUNKS * KB + (p * TT + t) * 2 + u + 1)
                    split_three_pass(xn_t[:, t % 2, 0, 4 * u:4 * u + 4, :].rearrange("p a n -> p (a n)"),
                                     xn_t[:, t % 2, 1, 4 * u:4 * u + 4, :].rearrange("p a n -> p (a n)"),
                                     ps[:, banks[u], :], t_moved)

            def add_dense(p, t, half, bank=SHARED):
                dve.wait_ge(yb_ready, p * TT + t + 1)
                dve.wait_ge(ffn_ready, START + (p * TT + t) * 2 + half + 1)
                nc.vector.tensor_tensor(y[:, t, bass.ts(half, N)], ps[:, bank, :], y[:, t, bass.ts(half, N)], ALU.add
                                        ).then_inc(ffn_moved, 1)

            for k in range(3):
                move_w(k)
            move_o(0, 0, True)
            move_w(3)
            norm_o(0, 0)
            for k in range(4, 2 * KB):
                move_w(k)
            with dve.Fori(1, CHUNKS) as c:
                p = c - 1
                move_o(p, 1)
                norm_o(p, 1)
                split_o(p)
                ch = Chain(v_ln)
                for t in range(TT):
                    residual(p, t, (SHARED, SHARED), ch)
                deviations(ch)
                dve.wait_ge(t_ready, START + CHUNKS * KB + p * UNITS)
                normalise()
                for t in range(TT):
                    move_xn(p, t, (SHARED, SHARED))
                    add_dense(p, t, 0)
                    if t == 1:
                        move_o(c, 0)
                    add_dense(p, t, 1)
                    if t == 1:
                        norm_o(c, 0)
            p = CHUNKS - 1
            move_o(p, 1)
            norm_o(p, 1)
            split_o(p)
            dve.wait_ge(t_ready, START + CHUNKS * KB + p * UNITS)
            for t in range(TT):
                ch = Chain(v_ln)
                residual(p, t, (2 * (t % 2), 2 * (t % 2) + 1), ch)
                deviations(ch, tiles=range(t, t + 1))
                normalise(range(t, t + 1))
                if t:
                    add_dense(p, t - 1, 0, 6)
                move_xn(p, t, (4, 5))
                if t:
                    add_dense(p, t - 1, 1, 7)
            for half in range(2):
                add_dense(p, TT - 1, half, 6 + half)


_INS = ["L0_attn_x", "L0_attn_Wq_d", "L0_attn_bq_d", "L0_attn_W_qk", "L0_attn_b_qk", "L0_attn_Wkv_d", "L0_attn_bkv_d",
        "L0_attn_Wv_u", "L0_attn_bv_u", "L0_attn_Wo", "L0_attn_bo", "L0_ffn_lora_A", "L0_ffn_lora_B", "L0_ffn_W",
        "L0_ffn_bias", "L0_ffn_lora_weights"]


def kernel(**inputs):
    import numpy as _np
    import concourse.bacc as _bacc
    from concourse import mybir as _mybir
    from concourse.bass_utils import run_bass_kernel_spmd as _run

    nc = _bacc.Bacc("TRN2", target_bir_lowering=False, num_devices=1)
    arrays, args = {}, []
    for name in _INS:
        a = _np.ascontiguousarray(inputs[name])
        arrays[f"in_{name}_dram"] = a
        args.append(nc.dram_tensor(f"in_{name}_dram", a.shape, _mybir.dt.from_np(a.dtype), kind="ExternalInput").ap())
    shape = inputs["L0_attn_x"].shape
    args.append(nc.dram_tensor("out_0_dram", shape, F32, kind="ExternalOutput").ap())
    build_block(nc, *args)
    r = _run(nc, [arrays], core_ids=[0])
    return r.results[0]["out_0_dram"]
```
